# Optimizing a Trainium2 kernel written in Bass

```python
import numpy as np
import jax
import jax.numpy as jnp

def _softmax(x, axis=-1):
    return jax.nn.softmax(x, axis=axis)

def _gelu(x):
    return jax.nn.gelu(x, approximate=True)

def _silu(x):
    return jax.nn.silu(x)

def _sigmoid(x):
    return jax.nn.sigmoid(x)

def _layernorm(x, axis=-1, eps=1e-05):
    m = jnp.mean(x, axis=axis, keepdims=True)
    v = jnp.var(x, axis=axis, keepdims=True)
    return (x - m) / jnp.sqrt(v + eps)

def _scatter_add(tgt, idx, src, axis=0):
    return tgt.at[idx].add(src)

def _segment_sum(src, seg, n):
    return jax.ops.segment_sum(src, seg, n)
kernel_name = 'mk_prb_d2_jaxref_r8_cf805b'

def setup_inputs(seed: int=0):
    np.random.seed(seed)
    _w = jnp.asarray

    def _L0_attn_setup():
        import jax, jax.numpy as jnp
        import numpy as np
        B_, L_, D_, N_, R_ = (2, 256, 256, 16, 64)
        DT_MIN, DT_MAX = (0.001, 0.1)
        key = jax.random.key(seed)
        k0, k1, k2, k3 = jax.random.split(key, 4)
        x = jax.random.normal(k0, (B_, L_, D_), jnp.float32)
        W_xproj = jax.random.normal(k1, (R_ + 2 * N_, D_), jnp.float32) * D_ ** (-0.5)
        dt_std = R_ ** (-0.5)
        W_dt = jax.random.uniform(k2, (D_, R_), jnp.float32, -dt_std, dt_std)
        dt = jnp.exp(jax.random.uniform(k3, (D_,), jnp.float32) * (np.log(DT_MAX) - np.log(DT_MIN)) + np.log(DT_MIN))
        b_dt = dt + jnp.log(-jnp.expm1(-dt))
        A_log = jnp.log(jnp.broadcast_to(jnp.arange(1, N_ + 1, dtype=jnp.float32), (D_, N_)))
        D_param = jnp.ones((D_,), jnp.float32)
        return dict(x=x, W_xproj=W_xproj, W_dt=W_dt, b_dt=b_dt, A_log=A_log, D_param=D_param)
    _L0_attn_in = _L0_attn_setup()

    def _L0_ffn_setup():
        import jax, jax.numpy as jnp
        import numpy as np
        B, S, H = (4, 128, 256)
        E, K, I, SI = (16, 4, 176, 704)

        def _silu_mul(gu, inter):
            return jax.nn.silu(gu[:, :inter]) * gu[:, inter:]
        key = jax.random.key(seed)
        ks = jax.random.split(key, 7)
        s = 0.02
        return {'hidden_states': jax.random.normal(ks[0], (B, S, H), jnp.float32), 'gate_w': jax.random.normal(ks[1], (E, H), jnp.float32) * s, 'expert_gate_up': jax.random.normal(ks[2], (E, 2 * I, H), jnp.float32) * s, 'expert_down': jax.random.normal(ks[3], (E, H, I), jnp.float32) * s, 'shared_gate_up': jax.random.normal(ks[4], (2 * SI, H), jnp.float32) * s, 'shared_down': jax.random.normal(ks[5], (H, SI), jnp.float32) * s, 'shared_gate_vec': jax.random.normal(ks[6], (1, H), jnp.float32) * s}
    _L0_ffn_in = _L0_ffn_setup()

    def _L1_attn_setup():
        import jax, jax.numpy as jnp
        import numpy as np
        B_, L_, D_MODEL = (2, 256, 256)
        EXPAND = 2
        D_IN = EXPAND * D_MODEL
        HEADS = 64
        HEAD_DIM = D_IN // HEADS
        STATE = 128
        NGROUPS = 1
        K = 4
        CONV_DIM = D_IN + 2 * NGROUPS * STATE
        PROJ = D_IN + CONV_DIM + HEADS
        CHUNK = 32
        EPS = 1e-05

        def _segsum(x):
            T = x.shape[-1]
            c = jnp.cumsum(x, axis=-1)
            seg = c[..., :, None] - c[..., None, :]
            return jnp.where(jnp.tril(jnp.ones((T, T), bool)), seg, -jnp.inf)

        def _ssd(x, dA, Bm, Cm):
            b, l, h, p = x.shape
            n = Bm.shape[-1]
            c = l // CHUNK
            rep = h // Bm.shape[2]
            Bh = jnp.repeat(Bm, rep, axis=2).reshape(b, c, CHUNK, h, n)
            Ch = jnp.repeat(Cm, rep, axis=2).reshape(b, c, CHUNK, h, n)
            x = x.reshape(b, c, CHUNK, h, p)
            dA = dA.reshape(b, c, CHUNK, h).transpose(0, 3, 1, 2)
            dA_cum = jnp.cumsum(dA, axis=-1)
            Lmat = jnp.exp(_segsum(dA))
            Y_diag = jnp.einsum('bcthn,bcshn,bhcts,bcshp->bcthp', Ch, Bh, Lmat, x)
            decay_states = jnp.exp(dA_cum[..., -1:] - dA_cum)
            states = jnp.einsum('bcshn,bhcs,bcshp->bchpn', Bh, decay_states, x)
            chunk_decay = jnp.exp(_segsum(jnp.pad(dA_cum[..., -1], ((0, 0), (0, 0), (1, 0)))))
            states = jnp.concatenate([jnp.zeros_like(states[:, :1]), states], axis=1)
            prev = jnp.einsum('bhzc,bchpn->bzhpn', chunk_decay, states)[:, :-1]
            Y_off = jnp.einsum('bcthn,bchpn,bhct->bcthp', Ch, prev, jnp.exp(dA_cum))
            return (Y_diag + Y_off).reshape(b, l, h, p)
        key = jax.random.key(seed)
        ks = jax.random.split(key, 4)
        return {'hidden_states': jax.random.normal(ks[0], (B_, L_, D_MODEL), jnp.float32), 'in_proj_w': jax.random.normal(ks[1], (PROJ, D_MODEL), jnp.float32) * 0.02, 'conv_w': jax.random.normal(ks[2], (CONV_DIM, K), jnp.float32) * 0.2, 'conv_b': jnp.zeros((CONV_DIM,), jnp.float32), 'dt_bias': jnp.ones((HEADS,), jnp.float32), 'A_log': jnp.log(jnp.arange(1, HEADS + 1, dtype=jnp.float32)), 'D': jnp.ones((HEADS,), jnp.float32), 'norm_w': jnp.ones((D_IN,), jnp.float32), 'out_proj_w': jax.random.normal(ks[3], (D_MODEL, D_IN), jnp.float32) * 0.02}
    _L1_attn_in = _L1_attn_setup()

    def _L1_ffn_setup():
        import jax, jax.numpy as jnp
        import numpy as np
        TOPK = 2

        def _mlp(x, w1, w2, w3):
            a = jnp.dot(x, w1.T).astype(jnp.float32)
            b = jnp.dot(x, w3.T).astype(jnp.float32)
            h = (jax.nn.silu(a) * b).astype(x.dtype)
            return jnp.dot(h, w2.T)
        key = jax.random.key(seed)
        ks = jax.random.split(key, 8)
        B, S, D, I, E = (4, 256, 256, 176, 16)
        SI = I * 2
        sc = 0.02
        return {'x': jax.random.normal(ks[0], (B, S, D), jnp.bfloat16), 'gate_w': jax.random.normal(ks[1], (E, D), jnp.float32) * sc, 'w1': jax.random.normal(ks[2], (E, I, D), jnp.bfloat16) * sc, 'w2': jax.random.normal(ks[3], (E, D, I), jnp.bfloat16) * sc, 'w3': jax.random.normal(ks[4], (E, I, D), jnp.bfloat16) * sc, 'sw1': jax.random.normal(ks[5], (SI, D), jnp.bfloat16) * sc, 'sw2': jax.random.normal(ks[6], (D, SI), jnp.bfloat16) * sc, 'sw3': jax.random.normal(ks[7], (SI, D), jnp.bfloat16) * sc}
    _L1_ffn_in = _L1_ffn_setup()
    _d = {'L0_attn_x': _L0_attn_in['x'], 'L0_attn_W_xproj': _L0_attn_in['W_xproj'], 'L0_attn_W_dt': _L0_attn_in['W_dt'], 'L0_attn_b_dt': _L0_attn_in['b_dt'], 'L0_attn_A_log': _L0_attn_in['A_log'], 'L0_attn_D_param': _L0_attn_in['D_param'], 'L0_ffn_gate_w': _L0_ffn_in['gate_w'], 'L0_ffn_expert_gate_up': _L0_ffn_in['expert_gate_up'], 'L0_ffn_expert_down': _L0_ffn_in['expert_down'], 'L0_ffn_shared_gate_up': _L0_ffn_in['shared_gate_up'], 'L0_ffn_shared_down': _L0_ffn_in['shared_down'], 'L0_ffn_shared_gate_vec': _L0_ffn_in['shared_gate_vec'], 'L1_attn_in_proj_w': _L1_attn_in['in_proj_w'], 'L1_attn_conv_w': _L1_attn_in['conv_w'], 'L1_attn_conv_b': _L1_attn_in['conv_b'], 'L1_attn_dt_bias': _L1_attn_in['dt_bias'], 'L1_attn_A_log': _L1_attn_in['A_log'], 'L1_attn_D': _L1_attn_in['D'], 'L1_attn_norm_w': _L1_attn_in['norm_w'], 'L1_attn_out_proj_w': _L1_attn_in['out_proj_w'], 'L1_ffn_gate_w': _L1_ffn_in['gate_w'], 'L1_ffn_w1': _L1_ffn_in['w1'], 'L1_ffn_w2': _L1_ffn_in['w2'], 'L1_ffn_w3': _L1_ffn_in['w3'], 'L1_ffn_sw1': _L1_ffn_in['sw1'], 'L1_ffn_sw2': _L1_ffn_in['sw2'], 'L1_ffn_sw3': _L1_ffn_in['sw3']}
    _x0 = _d['L0_attn_x']
    _d['L0_attn_x'] = jax.random.normal(jax.random.fold_in(jax.random.key(seed), 1), (4, 512, 256), dtype=_x0.dtype)
    del _x0
    return _d

def reference(L0_attn_x, L0_attn_W_xproj, L0_attn_W_dt, L0_attn_b_dt, L0_attn_A_log, L0_attn_D_param, L0_ffn_gate_w, L0_ffn_expert_gate_up, L0_ffn_expert_down, L0_ffn_shared_gate_up, L0_ffn_shared_down, L0_ffn_shared_gate_vec, L1_attn_in_proj_w, L1_attn_conv_w, L1_attn_conv_b, L1_attn_dt_bias, L1_attn_A_log, L1_attn_D, L1_attn_norm_w, L1_attn_out_proj_w, L1_ffn_gate_w, L1_ffn_w1, L1_ffn_w2, L1_ffn_w3, L1_ffn_sw1, L1_ffn_sw2, L1_ffn_sw3):

    def _L0_attn_ref(x, W_xproj, W_dt, b_dt, A_log, D_param):
        import jax, jax.numpy as jnp
        import numpy as np
        B_, L_, D_, N_, R_ = (2, 256, 256, 16, 64)
        DT_MIN, DT_MAX = (0.001, 0.1)
        R = W_dt.shape[1]
        N = A_log.shape[1]
        x_dbl = jnp.einsum('bld,ed->ble', x, W_xproj)
        delta_raw, Bm, Cm = jnp.split(x_dbl, [R, R + N], axis=-1)
        delta = jax.nn.softplus(jnp.einsum('blr,dr->bld', delta_raw, W_dt) + b_dt)
        A = -jnp.exp(A_log)
        dA = jnp.exp(jnp.einsum('bld,dn->bldn', delta, A))
        dBx = jnp.einsum('bld,bln->bldn', delta * x, Bm)

        def step(h, inp):
            dA_t, dBx_t, C_t = inp
            h = dA_t * h + dBx_t
            y_t = jnp.einsum('bdn,bn->bd', h, C_t)
            return (h, y_t)
        h0 = jnp.zeros((x.shape[0], x.shape[2], N), x.dtype)
        xs = (jnp.moveaxis(dA, 1, 0), jnp.moveaxis(dBx, 1, 0), jnp.moveaxis(Cm, 1, 0))
        _, ys = jax.lax.scan(step, h0, xs)
        y = jnp.moveaxis(ys, 0, 1)
        return y + x * D_param

    def _L0_ffn_ref(hidden_states, gate_w, expert_gate_up, expert_down, shared_gate_up, shared_down, shared_gate_vec):
        import jax, jax.numpy as jnp
        import numpy as np
        B, S, H = (4, 128, 256)
        E, K, I, SI = (16, 4, 176, 704)

        def _silu_mul(gu, inter):
            return jax.nn.silu(gu[:, :inter]) * gu[:, inter:]
        orig_shape = hidden_states.shape
        x = hidden_states.reshape(-1, H)
        router_logits = x @ gate_w.T
        routing_probs = jax.nn.softmax(router_logits.astype(jnp.float32), axis=-1)
        topk_w, topk_idx = jax.lax.top_k(routing_probs, K)
        topk_w = topk_w / topk_w.sum(axis=-1, keepdims=True)
        topk_w = topk_w.astype(x.dtype)
        combine = (jax.nn.one_hot(topk_idx, E, dtype=x.dtype) * topk_w[..., None]).sum(1)
        shared = _silu_mul(x @ shared_gate_up.T, SI) @ shared_down.T
        shared = shared * jax.nn.sigmoid(x @ shared_gate_vec.T)

        def step(acc, ew):
            w_gu, w_d, cw = ew
            h = _silu_mul(x @ w_gu.T, I)
            return (acc + h @ w_d.T * cw[:, None], None)
        acc0 = jnp.zeros_like(x)
        sparse, _ = jax.lax.scan(step, acc0, (expert_gate_up, expert_down, combine.T))
        return (shared + sparse).reshape(orig_shape)

    def _L1_attn_ref(hidden_states, in_proj_w, conv_w, conv_b, dt_bias, A_log, D, norm_w, out_proj_w):
        import jax, jax.numpy as jnp
        import numpy as np
        B_, L_, D_MODEL = (2, 256, 256)
        EXPAND = 2
        D_IN = EXPAND * D_MODEL
        HEADS = 64
        HEAD_DIM = D_IN // HEADS
        STATE = 128
        NGROUPS = 1
        K = 4
        CONV_DIM = D_IN + 2 * NGROUPS * STATE
        PROJ = D_IN + CONV_DIM + HEADS
        CHUNK = 32
        EPS = 1e-05

        def _segsum(x):
            T = x.shape[-1]
            c = jnp.cumsum(x, axis=-1)
            seg = c[..., :, None] - c[..., None, :]
            return jnp.where(jnp.tril(jnp.ones((T, T), bool)), seg, -jnp.inf)

        def _ssd(x, dA, Bm, Cm):
            b, l, h, p = x.shape
            n = Bm.shape[-1]
            c = l // CHUNK
            rep = h // Bm.shape[2]
            Bh = jnp.repeat(Bm, rep, axis=2).reshape(b, c, CHUNK, h, n)
            Ch = jnp.repeat(Cm, rep, axis=2).reshape(b, c, CHUNK, h, n)
            x = x.reshape(b, c, CHUNK, h, p)
            dA = dA.reshape(b, c, CHUNK, h).transpose(0, 3, 1, 2)
            dA_cum = jnp.cumsum(dA, axis=-1)
            Lmat = jnp.exp(_segsum(dA))
            Y_diag = jnp.einsum('bcthn,bcshn,bhcts,bcshp->bcthp', Ch, Bh, Lmat, x)
            decay_states = jnp.exp(dA_cum[..., -1:] - dA_cum)
            states = jnp.einsum('bcshn,bhcs,bcshp->bchpn', Bh, decay_states, x)
            chunk_decay = jnp.exp(_segsum(jnp.pad(dA_cum[..., -1], ((0, 0), (0, 0), (1, 0)))))
            states = jnp.concatenate([jnp.zeros_like(states[:, :1]), states], axis=1)
            prev = jnp.einsum('bhzc,bchpn->bzhpn', chunk_decay, states)[:, :-1]
            Y_off = jnp.einsum('bcthn,bchpn,bhct->bcthp', Ch, prev, jnp.exp(dA_cum))
            return (Y_diag + Y_off).reshape(b, l, h, p)
        b, l, _ = hidden_states.shape
        proj = hidden_states @ in_proj_w.T
        gate = proj[..., :D_IN]
        xBC = proj[..., D_IN:D_IN + CONV_DIM]
        dt = proj[..., D_IN + CONV_DIM:]
        xp = jnp.pad(xBC, ((0, 0), (K - 1, 0), (0, 0)))
        conv = conv_b + sum((conv_w[:, i] * xp[:, i:i + l, :] for i in range(K)))
        xBC = jax.nn.silu(conv)
        x = xBC[..., :D_IN].reshape(b, l, HEADS, HEAD_DIM)
        Bm = xBC[..., D_IN:D_IN + NGROUPS * STATE].reshape(b, l, NGROUPS, STATE)
        Cm = xBC[..., D_IN + NGROUPS * STATE:].reshape(b, l, NGROUPS, STATE)
        dt = jax.nn.softplus(dt + dt_bias)
        A = -jnp.exp(A_log)
        y = _ssd(x * dt[..., None], dt * A, Bm, Cm)
        y = y + D[None, None, :, None] * x
        y = y.reshape(b, l, D_IN)
        hg = y * jax.nn.silu(gate)
        var = jnp.mean(hg * hg, axis=-1, keepdims=True)
        y = hg * jax.lax.rsqrt(var + EPS) * norm_w
        return y @ out_proj_w.T

    def _L1_ffn_ref(x, gate_w, w1, w2, w3, sw1, sw2, sw3):
        import jax, jax.numpy as jnp
        import numpy as np
        TOPK = 2

        def _mlp(x, w1, w2, w3):
            a = jnp.dot(x, w1.T).astype(jnp.float32)
            b = jnp.dot(x, w3.T).astype(jnp.float32)
            h = (jax.nn.silu(a) * b).astype(x.dtype)
            return jnp.dot(h, w2.T)
        B, S, D = x.shape
        E = gate_w.shape[0]
        xf = x.reshape(-1, D)
        T = xf.shape[0]
        scores = jax.nn.sigmoid(jnp.dot(xf.astype(jnp.float32), gate_w.T))
        topv, topi = jax.lax.top_k(scores, TOPK)
        topv = topv / topv.sum(axis=-1, keepdims=True)
        dw = jnp.zeros((T, E), jnp.float32).at[jnp.arange(T)[:, None], topi].add(topv)
        y0 = _mlp(xf, sw1, sw2, sw3).astype(jnp.float32)

        def step(y, ws):
            e1, e2, e3, we = ws
            out = _mlp(xf, e1, e2, e3).astype(jnp.float32)
            return (y + out * we[:, None], None)
        y, _ = jax.lax.scan(step, y0, (w1, w2, w3, dw.T))
        return y.astype(x.dtype).reshape(B, S, D)
    x = L0_attn_x
    xn = _layernorm(x, axis=-1)
    x = x + _L0_attn_ref(xn, L0_attn_W_xproj, L0_attn_W_dt, L0_attn_b_dt, L0_attn_A_log, L0_attn_D_param) + _L0_ffn_ref(xn, L0_ffn_gate_w, L0_ffn_expert_gate_up, L0_ffn_expert_down, L0_ffn_shared_gate_up, L0_ffn_shared_down, L0_ffn_shared_gate_vec)
    xn = _layernorm(x, axis=-1)
    x = x + _L1_attn_ref(xn, L1_attn_in_proj_w, L1_attn_conv_w, L1_attn_conv_b, L1_attn_dt_bias, L1_attn_A_log, L1_attn_D, L1_attn_norm_w, L1_attn_out_proj_w) + _L1_ffn_ref(xn, L1_ffn_gate_w, L1_ffn_w1, L1_ffn_w2, L1_ffn_w3, L1_ffn_sw1, L1_ffn_sw2, L1_ffn_sw3)
    return x

_drawn_inputs = setup_inputs


def setup_inputs(seed=0):
    import zlib

    import numpy as np

    out = dict(_drawn_inputs(seed))
    spreads = {'L0_attn_D_param': (1.0, 0.2),
     'L1_attn_conv_b': (0.0, 0.1),
     'L1_attn_dt_bias': (1.0, 0.6),
     'L1_attn_D': (1.0, 0.2),
     'L1_attn_norm_w': (1.0, 0.2)}
    factors = {'L0_ffn_gate_w': 8.0,
     'L0_ffn_expert_gate_up': 8.0,
     'L0_ffn_expert_down': 8.0,
     'L0_ffn_shared_gate_up': 8.0,
     'L0_ffn_shared_down': 8.0,
     'L0_ffn_shared_gate_vec': 8.0,
     'L1_attn_A_log': 8.0,
     'L1_ffn_gate_w': 8.0,
     'L1_ffn_w1': 8.0,
     'L1_ffn_w2': 8.0,
     'L1_ffn_w3': 8.0,
     'L1_ffn_sw1': 6.098,
     'L1_ffn_sw2': 6.061,
     'L1_ffn_sw3': 6.044}
    for name, (base, spread) in spreads.items():
        noise = np.random.default_rng([zlib.crc32(name.encode()), seed]).standard_normal(out[name].shape)
        drawn = base * np.exp(spread * noise) if base else spread * noise
        out[name] = jnp.asarray(drawn.astype(out[name].dtype))
    for name, factor in factors.items():
        out[name] = (out[name] * factor).astype(out[name].dtype)
    return out
```

```python
from contextlib import ExitStack

import numpy as np

import concourse.bass as bass
from concourse import mybir

F32 = mybir.dt.float32
BF16 = mybir.dt.bfloat16
F16 = mybir.dt.float16
I32 = mybir.dt.int32
U32 = mybir.dt.uint32
ALU = mybir.AluOpType
ACT = mybir.ActivationFunctionType
X = mybir.AxisListType.X

P = 128
NB, L, D = 4, 512, 256
T = NB * L
TT = T // P
KD = D // P
E = 16
FI = 176
FH = FI // 2
EPS = 1e-5

N0, R0 = 16, 64
K0, SI0 = 4, 704
K1, SI1 = 2, 352
AHEAD = 2


def tiles_of(k):
    n = (T * k + E * (P - 1)) // P
    return n + n % 2


NT0, NT1 = tiles_of(K0), tiles_of(K1)
MAXT = NT0 + AHEAD
RING = (5, 4)


class Tally:

    def __init__(self, sem):
        self.sem, self.n, self.base = sem, 0, 0

    def done(self, ins):
        ins.then_inc(self.sem, 1)
        self.n += 1
        return self.now

    @property
    def now(self):
        return self.base + self.n

    def enter(self, i, per):
        self.start, self.per = self.n, per
        self.base, self.n = self.start + i * per, 0

    def leave(self, count):
        assert self.n == self.per, (self.n, self.per)
        self.base, self.n = 0, self.start + count * self.per



def build(nc, a, out):
    with ExitStack() as ctx:
        _program(nc, a, out, ctx)


def _program(nc, a, out, ctx):
    def sem(name):
        return ctx.enter_context(nc.semaphore(name))

    def sb(name, shape, dt=F32, at=ctx):
        return at.enter_context(nc.sbuf_tensor(name, shape, dt))

    bank = ctx.enter_context(nc.psum_tensor("bank", [P, 8, 512], F32))
    ident = sb("ident", [P, P])
    ones = sb("ones", [P, P])
    before = sb("before", [P, P])
    iota = sb("iota", [P, P])
    iota128 = sb("iota128", [P, E])
    token_id = sb("token_id", [P, TT])
    not_first = sb("not_first", [P, E, TT])
    x0 = sb("x0", [P, TT, D])
    xnT = sb("xnT", [P, KD, T])
    stats = sb("stats", [P, TT, 6])
    ln = sb("ln", [P, 6, TT])
    weight = sb("weight", [P, TT, K0])
    slot_i = sb("slot_i", [P, TT, K0], I32)
    token_i = sb("token_i", [P, MAXT], I32)
    expert_i = sb("expert_i", [P, MAXT], I32)
    xg = sb("xg", [P, 5, D])
    xgT = sb("xgT", [P, 2, KD, P])
    act_t = sb("act_t", [P, 2, FI])
    hid = sb("hid", [P, 2, FI])
    hidT = sb("hidT", [FH, 2, 2, P])
    yo = sb("yo", [P, 5, D])

    xn_d = [nc.dram_tensor(f"xn_d{l}", (T, D), F32).ap() for l in range(2)]
    y_d = [nc.dram_tensor(f"y_d{l}", (n * P, D), F32).ap() for l, n in enumerate((NT0, NT1))]

    consts_ready = sem("consts_ready")
    x_loaded = sem("x_loaded")
    out_stored = sem("out_stored")
    vec, sca, poo = Tally(sem("vec")), Tally(sem("sca")), Tally(sem("poo"))

    waits_apart = sem("waits_apart")

    def apart(eng):
        eng.sem_inc(waits_apart, 1)

    class Layer:

        def __init__(self, l):
            self.rms_in, self.rms_out, self.xn_rows = sem(f"rms_in{l}"), sem(f"rms_out{l}"), sem(f"xn_rows{l}")
            self.xn_stored, self.tr_full, self.tr_free = sem(f"xn_stored{l}"), sem(f"tr_full{l}"), sem(f"tr_free{l}")
            self.logits, self.score_in, self.score_out = sem(f"logits{l}"), sem(f"score_in{l}"), sem(f"score_out{l}")
            self.score2_in, self.mask_ready, self.ranks = sem(f"score2_in{l}"), sem(f"mask_ready{l}"), sem(f"ranks{l}")
            self.onehots, self.tokens, self.indices = sem(f"onehots{l}"), sem(f"tokens{l}"), sem(f"indices{l}")
            self.w_router, self.w_shared, self.pads = sem(f"w_router{l}"), sem(f"w_shared{l}"), sem(f"pads{l}")
            self.w_expert = sem(f"w_expert{l}")
            self.sh_in, self.sh_tanh, self.sh_out = sem(f"sh_in{l}"), sem(f"sh_tanh{l}"), sem(f"sh_out{l}")
            self.sh_free, self.sh_pfree = sem(f"sh_free{l}"), sem(f"sh_pfree{l}")
            self.xT_full, self.xT_ready, self.gu_full = sem(f"xT_full{l}"), sem(f"xT_ready{l}"), sem(f"gu_full{l}")
            self.tanh_ready, self.hid_ready, self.hT_full = sem(f"tanh_ready{l}"), sem(f"hid_ready{l}"), sem(f"hT_full{l}")
            self.hT_ready, self.y_full, self.y_ready = sem(f"hT_ready{l}"), sem(f"y_full{l}"), sem(f"y_ready{l}")
            self.experts_done, self.y_sum = sem(f"experts_done{l}"), sem(f"y_sum{l}")
            self.gathered = [sem(f"gathered{l}_{s}") for s in range(RING[l])]
            self.stored = [sem(f"stored{l}_{s}") for s in range(RING[l])]
            self.rows = [sem(f"rows{l}_{s}") for s in range(4)]

    ly = [Layer(0), Layer(1)]

    def layernorm_vector(v, l, xn):
        s = ly[l]
        for t in range(TT):
            last = vec.done(nc.vector.bn_stats(stats[:, t, :], x0[:, t, :]))
        v.wait_ge(vec.sem, last)
        mean, var, t0, t1, r, t2 = (ln[:, k, :] for k in range(6))
        vec.done(nc.vector.tensor_tensor(t0, stats[:, :, 1], stats[:, :, 4], ALU.add))
        vec.done(nc.vector.tensor_tensor(t1, stats[:, :, 1], stats[:, :, 4], ALU.subtract))
        vec.done(nc.vector.tensor_tensor(t2, stats[:, :, 2], stats[:, :, 5], ALU.add))
        v.wait_ge(vec.sem, vec.now)
        vec.done(nc.vector.tensor_scalar(mean, t0, 0.5, None, ALU.mult))
        vec.done(nc.vector.tensor_tensor(t1, t1, t1, ALU.mult))
        vec.done(nc.vector.tensor_scalar(t2, t2, 1.0 / D, EPS, ALU.mult, ALU.add))
        v.wait_ge(vec.sem, vec.now)
        nc.vector.scalar_tensor_tensor(var, t1, 0.25, t2, ALU.mult, ALU.add).then_inc(s.rms_in, 1)
        v.wait_ge(s.rms_out, 1)
        vec.done(nc.vector.tensor_tensor(t0, r, r, ALU.mult))
        v.wait_ge(vec.sem, vec.now)
        vec.done(nc.vector.tensor_tensor(t0, t0, var, ALU.mult))
        v.wait_ge(vec.sem, vec.now)
        vec.done(nc.vector.tensor_scalar(t0, t0, -0.5, 1.5, ALU.mult, ALU.add))
        v.wait_ge(vec.sem, vec.now)
        vec.done(nc.vector.tensor_tensor(r, r, t0, ALU.mult))
        v.wait_ge(vec.sem, vec.now)
        for t in range(TT):
            nc.vector.tensor_scalar(xn[:, t, :], x0[:, t, :], mean[:, t:t + 1], r[:, t:t + 1],
                                    ALU.subtract, ALU.mult).then_inc(s.xn_rows, 1)

    def layernorm_scalar(act, l):
        s = ly[l]
        act.wait_ge(s.rms_in, 1)
        sca.done(nc.scalar.activation(ln[:, 2, :], ln[:, 1, :], ACT.Ln))
        act.wait_ge(sca.sem, sca.now)
        nc.scalar.activation(ln[:, 4, :], ln[:, 2, :], ACT.Exp, scale=-0.5).then_inc(s.rms_out, 1)
        for g in range(KD * TT // 4):
            k, q = g % KD, g // KD
            act.wait_ge(s.tr_full, g + 1)
            nc.scalar.activation(xnT[:, k, q * 512:(q + 1) * 512], bank[:, g % 4, :], ACT.Copy).then_inc(s.tr_free, 1)

    def layernorm_tensor(pe, l, xn):
        s = ly[l]
        if l == 0:
            pe.wait_ge(consts_ready, 1)
        for g in range(KD * TT // 4):
            k, q = g % KD, g // KD
            pe.wait_ge(s.xn_rows, 4 * q + 4)
            if g >= 4:
                pe.wait_ge(s.tr_free, g - 3)
            for j in range(4):
                last = nc.tensor.transpose(bank[:, g % 4, j * P:(j + 1) * P], xn[:, 4 * q + j, k * P:(k + 1) * P], ident[:, :])
            last.then_inc(s.tr_full, 1)

    def layernorm_sync(sp, l, xn):
        s = ly[l]
        sp.wait_ge(s.xn_rows, TT)
        sp.dma_start(xn_d[l].rearrange("(t p) d -> p t d", p=P), xn[:, :, :]).then_inc(s.xn_stored, 16)

    def route_tensor(pe, l, K, wr, nr, m):
        s = ly[l]
        NT = (NT0, NT1)[l] + AHEAD
        pe.wait_ge(s.tr_free, KD * TT // 4)
        pe.wait_ge(s.w_router, 16 * (2 - l))
        for t in range(TT):
            for k in range(KD):
                last = nc.tensor.matmul(bank[:, 4, t * nr:(t + 1) * nr], xnT[:, k, t * P:(t + 1) * P], wr[:, k, :],
                                        start=(k == 0), stop=(k == KD - 1))
        last.then_inc(s.logits, 1)
        pe.wait_ge(s.mask_ready, 1)
        nc.tensor.matmul(bank[:, 5, 0:TT * E], before[:, :], m["mask"], start=True, stop=True).then_inc(s.ranks, 1)
        nc.tensor.matmul(bank[:, 6, 0:TT * E], ones[:, :], m["mask"], start=True, stop=True).then_inc(s.ranks, 1)
        pe.wait_ge(s.onehots, 1)
        for n in range(TT * K):
            last = nc.tensor.matmul(bank[:, 7, 0:NT], m["row_1h"][:, n, :], m["tile_1h"][:, n, :],
                                    start=(n == 0), stop=(n == TT * K - 1))
        last.then_inc(s.tokens, 1)

    def route_scalar(act, l, m):
        s = ly[l]
        act.wait_ge(s.score_in, 1)
        nc.scalar.activation(m["score"], m["score"], ACT.Exp, scale=(1.0, -1.0)[l]).then_inc(s.score_out, 1)

    def route_vector(v, l, K, nr, m):
        s = ly[l]
        NT = (NT0, NT1)[l] + AHEAD
        logits, score, top, top_i, idx = m["logits"], m["score"], m["top"], m["top_i"], m["idx"]
        v.wait_ge(s.logits, 1)
        nc.vector.tensor_copy(logits, bank[:, 4, 0:TT * nr].rearrange("p (t n) -> p t n", n=nr)).then_inc(s.logits, 1)
        v.wait_ge(s.logits, 2)
        if l == 0:
            vec.done(nc.vector.tensor_reduce(m["mx"], logits[:, :, 0:E], X, ALU.max))
            v.wait_ge(vec.sem, vec.now)
            nc.vector.tensor_tensor(score, logits[:, :, 0:E], m["mx"].unsqueeze(2).to_broadcast([P, TT, E]),
                                    ALU.subtract).then_inc(s.score_in, 1)
        else:
            nc.vector.tensor_copy(score, logits[:, :, 0:E]).then_inc(s.score_in, 1)
        v.wait_ge(s.score_out, 1)
        if l == 1:
            vec.done(nc.vector.tensor_scalar(score, score, 1.0, None, ALU.add))
            v.wait_ge(vec.sem, vec.now)
            vec.done(nc.vector.reciprocal(score, score))
            v.wait_ge(vec.sem, vec.now)
        for t in range(TT):
            vec.done(nc.vector.max(top[:, t, :], score[:, t, :]))
        v.wait_ge(vec.sem, vec.now)
        for t in range(TT):
            vec.done(nc.vector.max_index(top_i[:, t, :], top[:, t, :], score[:, t, :]))
        vec.done(nc.vector.tensor_reduce(m["mx"], top[:, :, 0:K], X, ALU.add))
        v.wait_ge(vec.sem, vec.now)
        vec.done(nc.vector.reciprocal(m["mx"], m["mx"]))
        vec.done(nc.vector.tensor_copy(idx, top_i[:, :, 0:K]))
        v.wait_ge(vec.sem, vec.now)
        vec.done(nc.vector.tensor_tensor(weight[:, :, 0:K], top[:, :, 0:K],
                                         m["mx"].unsqueeze(2).to_broadcast([P, TT, K]), ALU.mult))
        chosen = m["chosen"]
        flat = chosen.rearrange("p t k e -> p (t k) e")
        vec.done(nc.vector.tensor_tensor(flat, idx.rearrange("p t k -> p (t k)").unsqueeze(2).to_broadcast([P, TT * K, E]),
                                         iota[:, None, 0:E].to_broadcast([P, TT * K, E]), ALU.is_equal))
        v.wait_ge(vec.sem, vec.now)
        nc.vector.tensor_reduce(m["mask"].rearrange("p (t e) -> p t e", e=E), chosen.rearrange("p t k e -> p t e k"),
                                X, ALU.add).then_inc(s.mask_ready, 1)
        v.wait_ge(s.ranks, 2)
        tot, incl, pos = m["tot"], m["incl"], m["pos"]
        vec.done(nc.vector.tensor_copy(tot, bank[:, 6, 0:TT * E].rearrange("p (t e) -> p e t", e=E)))
        v.wait_ge(vec.sem, vec.now)
        vec.done(nc.vector.tensor_tensor_scan(incl.rearrange("p e t -> p (e t)"), not_first[:, :, :].rearrange("p e t -> p (e t)"),
                                              tot.rearrange("p e t -> p (e t)"), 0.0, ALU.mult, ALU.add))
        v.wait_ge(vec.sem, vec.now)
        vec.done(nc.vector.tensor_tensor(m["cmp"], incl[:, :, TT - 1:TT].to_broadcast([P, E, E]),
                                         iota128[:, None, :].to_broadcast([P, E, E]), ALU.is_gt))
        vec.done(nc.vector.tensor_tensor(pos, incl, tot, ALU.subtract))
        v.wait_ge(vec.sem, vec.now)
        vec.done(nc.vector.tensor_reduce(m["ntile"], m["cmp"], X, ALU.add))
        v.wait_ge(vec.sem, vec.now)
        vec.done(nc.vector.tensor_tensor_scan(m["tile_end"], ones[:, 0:E], m["ntile"], 0.0, ALU.mult, ALU.add))
        v.wait_ge(vec.sem, vec.now)
        vec.done(nc.vector.tensor_tensor(m["ntile"], m["tile_end"], m["ntile"], ALU.subtract))
        vec.done(nc.vector.tensor_tensor(m["q_cmp"], m["tile_end"].unsqueeze(1).to_broadcast([P, NT, E]),
                                         iota[:, 0:NT, None].to_broadcast([P, NT, E]), ALU.is_le))
        v.wait_ge(vec.sem, vec.now)
        vec.done(nc.vector.tensor_reduce(m["q_sum"], m["q_cmp"], X, ALU.add))
        vec.done(nc.vector.scalar_tensor_tensor(pos, m["ntile"].unsqueeze(2).to_broadcast([P, E, TT]), float(P), pos,
                                                ALU.mult, ALU.add))
        v.wait_ge(vec.sem, vec.now)
        vec.done(nc.vector.tensor_scalar(expert_i[:, 0:NT], m["q_sum"], float(E - 1), None, ALU.min))
        vec.done(nc.vector.tensor_tensor(m["pos_t"], pos.rearrange("p e t -> p t e"),
                                         bank[:, 5, 0:TT * E].rearrange("p (t e) -> p t e", e=E), ALU.add))
        v.wait_ge(vec.sem, vec.now)
        for k in range(K):
            vec.done(nc.vector.tensor_tensor(chosen[:, :, k, :], chosen[:, :, k, :], m["pos_t"], ALU.mult))
        v.wait_ge(vec.sem, vec.now)
        slot = m["slot"]
        vec.done(nc.vector.tensor_reduce(slot, flat, X, ALU.add))
        v.wait_ge(vec.sem, vec.now)
        vec.done(nc.vector.tensor_copy(m["slot_c"], slot.rearrange("p (t k) -> p t k", k=K)))
        v.wait_ge(vec.sem, vec.now)
        vec.done(nc.vector.tensor_copy(slot_i[:, :, 0:K], m["slot_c"]))
        vec.done(nc.vector.tensor_scalar(m["row_i"], m["slot_c"].rearrange("p t k -> p (t k)"), P - 1, None, ALU.bitwise_and))
        vec.done(nc.vector.tensor_scalar(m["tile_i"], m["slot_c"].rearrange("p t k -> p (t k)"), 7, None, ALU.logical_shift_right))
        v.wait_ge(vec.sem, vec.now)
        vec.done(nc.vector.tensor_copy(m["row_f"], m["row_i"]))
        vec.done(nc.vector.tensor_copy(m["tile_f"], m["tile_i"]))
        v.wait_ge(vec.sem, vec.now)
        n = TT * K
        vec.done(nc.vector.tensor_tensor(m["row_1h"], m["row_f"].unsqueeze(2).to_broadcast([P, n, P]),
                                         iota[:, None, :].to_broadcast([P, n, P]), ALU.is_equal))
        vec.done(nc.vector.tensor_tensor(m["tile_1h"], m["tile_f"].unsqueeze(2).to_broadcast([P, n, NT]),
                                         iota[:, None, 0:NT].to_broadcast([P, n, NT]), ALU.is_equal))
        v.wait_ge(vec.sem, vec.now)
        by_token = m["tile_1h"].rearrange("p (t k) q -> p t (k q)", k=K)
        nc.vector.tensor_tensor(by_token, by_token,
                                token_id[:, :, None].to_broadcast([P, TT, K * NT]), ALU.mult).then_inc(s.onehots, 1)
        v.wait_ge(s.tokens, 1)
        nc.vector.tensor_copy(token_i[:, 0:NT], bank[:, 7, 0:NT]).then_inc(s.indices, 1)

    def route_memory(scr, l, K, nr):
        NT = (NT0, NT1)[l] + AHEAD
        at = [0]

        def take(n, dt=F32):
            words = n if dt in (F32, I32, U32) else (n + 1) // 2
            v = scr[:, at[0]:at[0] + words]
            at[0] += words
            return v if dt == F32 else v.bitcast(dt)[:, 0:n]

        m = {}
        m["logits"] = take(TT * nr).rearrange("p (t n) -> p t n", n=nr)
        m["score"] = take(TT * E).rearrange("p (t n) -> p t n", n=E)
        m["mx"] = take(TT)
        m["top"] = take(TT * 8).rearrange("p (t n) -> p t n", n=8)
        m["top_i"] = take(TT * 8, U32).rearrange("p (t n) -> p t n", n=8)
        m["idx"] = take(TT * K).rearrange("p (t k) -> p t k", k=K)
        m["chosen"] = take(TT * K * E).rearrange("p (t k e) -> p t k e", k=K, e=E)
        m["mask"] = take(TT * E)
        for name in ("tot", "incl", "pos"):
            m[name] = take(TT * E).rearrange("p (e t) -> p e t", t=TT)
        m["pos_t"] = take(TT * E).rearrange("p (t e) -> p t e", e=E)
        m["cmp"] = take(E * E).rearrange("p (e j) -> p e j", j=E)
        m["ntile"], m["tile_end"] = take(E), take(E)
        m["q_cmp"] = take(NT * E).rearrange("p (q e) -> p q e", e=E)
        m["q_sum"] = take(NT)
        m["slot"], m["row_f"], m["tile_f"] = take(TT * K), take(TT * K), take(TT * K)
        m["slot_c"] = take(TT * K, I32).rearrange("p (t k) -> p t k", k=K)
        m["row_i"], m["tile_i"] = take(TT * K, I32), take(TT * K, I32)
        m["row_1h"] = take(TT * K * P, F16).rearrange("p (n r) -> p n r", r=P)
        m["tile_1h"] = take(TT * K * NT, F16).rearrange("p (n q) -> p n q", q=NT)
        m["words"] = at[0]
        return m

    def shared_tensor(pe, l, F, sg, su, sd, shT):
        s = ly[l]
        pe.wait_ge(s.w_shared, 64)
        pe.wait_ge(s.pads, 1)
        pe.wait_ge(s.tr_free, KD * TT // 4)
        with pe.Fori(0, NB) as c:
            for f in range(F):
                pe.wait_ge(s.sh_free, c * F + f + 1)
                g = 2 * (f % 2)
                for w, b in ((sg, g), (su, g + 1)):
                    for k in range(KD):
                        last = nc.tensor.matmul(bank[:, b, :], w[:, k, f * P:(f + 1) * P], xnT[:, k, bass.ds(c * 512, 512)],
                                                start=(k == 0), stop=(k == KD - 1))
                last.then_inc(s.sh_in, 1)
            pe.wait_ge(s.sh_free, c * F + F + 2)
            for j in range(4):
                pe.wait_ge(s.sh_pfree, c * 4 + j + 1)
                for f in range(F):
                    last = nc.tensor.matmul(bank[:, 4 + j, 0:D], shT[:, f, j * P:(j + 1) * P], sd[:, f, :],
                                            start=(f == 0), stop=(f == F - 1))
                last.then_inc(s.sh_out, 1)
        pe.wait_ge(s.sh_pfree, NB * 4 + 4)

    def shared_scalar(act, l, F, th):
        s = ly[l]
        with act.Fori(0, NB) as c:
            for f in range(F):
                act.wait_ge(s.sh_in, c * F + f + 1)
                act.wait_ge(s.sh_free, c * F + f + 1)
                nc.scalar.activation(th[:, f % 2, :], bank[:, 2 * (f % 2), :], ACT.Tanh, scale=0.5).then_inc(s.sh_tanh, 1)


    def shared_vector(v, l, F, th, shT, scale):
        s = ly[l]
        with v.Fori(0, NB) as c:
            vec.enter(c, F)
            for f in range(F):
                g = 2 * (f % 2)
                v.wait_ge(s.sh_tanh, c * F + f + 1)
                vec.done(nc.vector.scalar_tensor_tensor(th[:, f % 2, :], th[:, f % 2, :], 1.0, bank[:, g, :], ALU.add, ALU.mult))
                v.wait_ge(vec.sem, vec.now)
                nc.vector.scalar_tensor_tensor(shT[:, f, :], th[:, f % 2, :], 0.5, bank[:, g + 1, :],
                                               ALU.mult, ALU.mult).then_inc(s.sh_free, 1)
            for j in range(4):
                v.wait_ge(s.sh_out, c * 4 + j + 1)
                xt = x0[:, bass.ds(c * 4 + j, 1), :].rearrange("p a d -> p (a d)")
                if scale is None:
                    nc.vector.tensor_tensor(xt, bank[:, 4 + j, 0:D], xt, ALU.add).then_inc(s.sh_pfree, 1)
                else:
                    nc.vector.scalar_tensor_tensor(xt, bank[:, 4 + j, 0:D], scale[:, bass.ds(c * 4 + j, 1)], xt,
                                                   ALU.mult, ALU.add).then_inc(s.sh_pfree, 1)
            vec.leave(NB)

    def expert_gather(pool, l, n_tiles):
        s = ly[l]
        pool.wait_ge(s.indices, 1)
        pool.wait_ge(s.xn_stored, 16)
        for q in range(n_tiles + AHEAD):
            if q >= RING[l]:
                pool.wait_ge(s.xT_full, q - RING[l] + 1)
            nc.gpsimd.indirect_dma_start(xg[:, q % RING[l], :], None, xn_d[l],
                                         bass.IndirectOffsetOnAxis(ap=token_i[:, q:q + 1], axis=0)).then_inc(s.gathered[q % RING[l]], 16)

    def x_transposes(pe, l, q, slot, count):
        s = ly[l]
        pe.wait_ge(s.gathered[slot], 16 * count)
        for k in range(KD):
            last = nc.tensor.transpose(bank[:, 4, k * P:(k + 1) * P], xg[:, slot, k * P:(k + 1) * P], ident[:, :])
        last.then_inc(s.xT_full, 1)

    def gate_up(pe, l, q, par, wgu):
        s = ly[l]
        e = pe.value_load(expert_i[0:1, bass.ds(q, 1)], min_val=0, max_val=E - 1)
        pe.wait_ge(s.xT_ready, q + 1)
        for k in range(KD):
            last = nc.tensor.matmul(bank[:, 2 + par, 0:2 * FI], xgT[:, par, k, :],
                                    wgu[:, k, bass.ds(e, 1), :].rearrange("p a f -> p (a f)"), start=(k == 0), stop=(k == KD - 1))
        last.then_inc(s.gu_full, 1)

    def down(pe, l, q, par, wd):
        s = ly[l]
        pe.wait_ge(s.hid_ready, q + 1)
        for h in range(2):
            last = nc.tensor.transpose(bank[0:FH, 5, h * P:(h + 1) * P], hid[:, par, h * FH:(h + 1) * FH], ident[:, :])
        last.then_inc(s.hT_full, 1)

        def product():
            e = pe.value_load(expert_i[0:1, bass.ds(q, 1)], min_val=0, max_val=E - 1)
            pe.wait_ge(s.hT_ready, q + 1)
            pe.wait_ge(s.y_ready, q + 1)
            for h in range(2):
                last = nc.tensor.matmul(bank[:, 6 + par, 0:D], hidT[:, par, h, :],
                                        wd[:, h, bass.ds(e, 1), :].rearrange("p a f -> p (a f)"), start=(h == 0), stop=(h == 1))
            last.then_inc(s.y_full, 1)
        return product

    def xT_copy(act, l, q, par):
        s = ly[l]
        act.wait_ge(s.xT_full, q + 1)
        nc.scalar.activation(xgT[:, par, :, :], bank[:, 4, 0:KD * P].rearrange("p (k t) -> p k t", k=KD), ACT.Copy).then_inc(s.xT_ready, 1)

    def gate_tanh(act, l, q, par):
        s = ly[l]
        act.wait_ge(s.gu_full, q + 1)
        nc.scalar.activation(act_t[:, par, :], bank[:, 2 + par, 0:FI], ACT.Tanh, scale=0.5).then_inc(s.tanh_ready, 1)

    def hT_copy(act, l, q, par):
        s = ly[l]
        act.wait_ge(s.hT_full, q + 1)
        nc.scalar.activation(hidT[:, par, :, :], bank[0:FH, 5, 0:2 * P].rearrange("p (k t) -> p k t", k=2), ACT.Copy).then_inc(s.hT_ready, 1)

    def y_copy(act, l, q, par, slot, count):
        s = ly[l]
        act.wait_ge(s.y_full, q + 1)
        act.wait_ge(s.stored[slot], 16 * count)
        nc.scalar.activation(yo[:, slot, :], bank[:, 6 + par, 0:D], ACT.Copy).then_inc(s.y_ready, 1)

    def silu_first(v, l, q, par):
        s = ly[l]
        v.wait_ge(s.tanh_ready, q + 1)
        vec.done(nc.vector.scalar_tensor_tensor(act_t[:, par, :], act_t[:, par, :], 1.0, bank[:, 2 + par, 0:FI], ALU.add, ALU.mult))

    def silu_second(v, l, q, par):
        s = ly[l]
        nc.vector.scalar_tensor_tensor(hid[:, par, :], act_t[:, par, :], 0.5, bank[:, 2 + par, FI:2 * FI],
                                       ALU.mult, ALU.mult).then_inc(s.hid_ready, 1)

    def y_store(sp, l, q, slot):
        s = ly[l]
        sp.wait_ge(s.y_ready, q + 1 + 2)
        sp.dma_start(y_d[l][bass.ds(q * P, P), :], yo[:, slot, :]).then_inc(s.stored[slot], 16)

    LB = 2 * L
    UN = N0 * 4
    with ExitStack() as c0:
        areaA = sb("areaA0", [P, (KD * 2 * FI + 2 * D) * E], F32, c0)
        wgu0 = areaA[:, 0:KD * E * 2 * FI].rearrange("p (k e f) -> p k e f", k=KD, e=E)
        wd0 = areaA[0:FH, KD * E * 2 * FI:].rearrange("p (h e d) -> p h e d", h=2, e=E)
        xn_tok = areaA[:, 0:TT * D].rearrange("p (t d) -> p t d", t=TT)
        m0 = route_memory(areaA[:, TT * D:], 0, K0, E + 1)
        areaB = sb("areaB0", [P, 5632], F32, c0)
        F0 = -(-SI0 // P)
        sg0 = areaB[:, 0:KD * F0 * P].rearrange("p (k f) -> p k f", k=KD)
        su0 = areaB[:, KD * F0 * P:2 * KD * F0 * P].rearrange("p (k f) -> p k f", k=KD)
        sd0 = areaB[:, 2 * KD * F0 * P:2 * KD * F0 * P + F0 * D].rearrange("p (f d) -> p f d", f=F0)
        th0 = areaB[:, 4608:4608 + 1024].rearrange("p (b t) -> p b t", b=2)
        dA = areaB[:, 0:2 * LB].rearrange("p (b t) -> p b t", b=2)
        h = areaB[:, 2 * LB:3 * LB]
        wr0 = sb("wr0", [P, KD, E + 1], F32, c0)
        wbc = sb("wbc", [P, KD, 3, 2 * N0], F32, c0)
        wdr = sb("wdr", [P, KD, R0], F32, c0)
        wdt = sb("wdt", [R0, D], F32, c0)
        b_dt = sb("b_dt", [P, 2], F32, c0)
        d_par = sb("d_par", [P, 2], F32, c0)
        a_neg = sb("a_neg", [P, 2, N0 + 1], F32, c0)
        sgate = sb("sgate", [P, TT], F32, c0)
        pick = sb("pick", [3 * 2 * N0, 2 * N0 + 4], BF16, c0)
        parts = sb("parts", [3 * 2 * N0, T], BF16, c0)
        delta = sb("delta", [P, 2, T], F32, c0)
        dx = sb("dx", [P, 2, T], F32, c0)
        y = sb("y", [P, 2, T], F32, c0)
        shT0 = y[:, :, :].rearrange("p h t -> p (h t)")[:, 0:F0 * 512].rearrange("p (f t) -> p f t", f=F0)
        bc = xnT[:, :, :].rearrange("p k (b t) -> p (k b) t", t=LB)
        rows = delta[:, :, :].rearrange("p h t -> p (h t)").rearrange("p (r k d) -> p r k d", r=4, d=D)
        drT = areaA[0:R0, TT * D + m0["words"]:TT * D + m0["words"] + T]
        v0 = areaB[:, 0:512]

        s = ly[0]
        w_scan = sem("w_scan")
        row_full, row_free, rank_ready = sem("row_full"), sem("row_free"), sem("rank_ready")
        z_full, z_exp, z_free, neg_a = sem("z_full"), sem("z_exp"), sem("z_free"), sem("neg_a")
        y_init, da_ready, da_free, bc_full, bc_ready, pair_free = (
            sem(n) for n in ("y_init", "da_ready", "da_free", "bc_full", "bc_ready", "pair_free"))
        yT_full, yT_free = sem("yT_full"), sem("yT_free")

        def scan_rows_tensor(pe):
            pe.wait_ge(w_scan, 16 * 7)
            pe.wait_ge(s.tr_free, KD * TT // 4)
            with pe.Fori(0, NB) as c:
                pe.wait_ge(row_free, c + 1)
                pe.wait_ge(rank_ready, c + 1)
                for k in range(KD):
                    nc.tensor.matmul(bank[0:96, 0, :], wbc[:, k, :, :].rearrange("p r n -> p (r n)"),
                                     xnT[:, k, bass.ds(c * 512, 512)], start=(k == 0), stop=(k == KD - 1))
                for k in range(KD):
                    last = nc.tensor.matmul(bank[0:R0, 1, :], wdr[:, k, :], xnT[:, k, bass.ds(c * 512, 512)],
                                            start=(k == 0), stop=(k == KD - 1))
                last.then_inc(row_full, 1)
            with pe.Fori(0, NB) as c:
                pe.wait_ge(rank_ready, c + 2)
                for hf in range(2):
                    pe.wait_ge(z_free, c * 2 + hf + 1)
                    apart(pe)
                    nc.tensor.matmul(bank[:, 2 + hf, :], wdt[:, hf * P:(hf + 1) * P], drT[:, bass.ds(c * 512, 512)],
                                     start=True, stop=True).then_inc(z_full, 1)

        def scan_rows_scalar(act):
            act.wait_ge(w_scan, 16 * 7)
            with act.Fori(0, NB) as c:
                act.wait_ge(row_full, c + 1)
                nc.scalar.activation(drT[:, bass.ds(c * 512, 512)], bank[0:R0, 1, :], ACT.Copy).then_inc(rank_ready, 1)
            nc.scalar.activation(a_neg[:, :, 0:N0], a_neg[:, :, 0:N0], ACT.Exp).then_inc(neg_a, 1)
            with act.Fori(0, NB) as c:
                sca.enter(c, 4)
                at = bass.ds(c * 512, 512)
                for hf in range(2):
                    act.wait_ge(z_full, c * 2 + hf + 1)
                    sca.done(nc.scalar.activation(delta[:, hf, at], bank[:, 2 + hf, :], ACT.Abs, bias=b_dt[:, hf:hf + 1]))
                    act.wait_ge(sca.sem, sca.now)
                    sca.done(nc.scalar.activation(dx[:, hf, at], delta[:, hf, at], ACT.Exp, scale=-1.0))
                    act.wait_ge(sca.sem, sca.now)
                    nc.scalar.activation(y[:, hf, at], dx[:, hf, at], ACT.Ln, bias=1.0).then_inc(z_exp, 1)
                sca.leave(NB)

        def scan_rows_vector(v):
            v.wait_ge(w_scan, 16 * 7)
            rest = areaB[:, 0:512]
            mid = areaB[:, 512:768].bitcast(BF16)
            with v.Fori(0, NB) as c:
                vec.enter(c, 5)
                at = bass.ds(c * 512, 512)
                v.wait_ge(row_full, c + 1)
                vec.done(nc.vector.tensor_copy(parts[:, at], bank[0:96, 0, :]))
                v.wait_ge(vec.sem, vec.now)
                nc.vector.tensor_tensor(rest[0:96, :], bank[0:96, 0, :], parts[:, at], ALU.subtract).then_inc(row_free, 1)
                v.wait_ge(row_free, c + 2)
                vec.done(nc.vector.tensor_copy(parts[32:64, at], rest[32:64, :]))
                vec.done(nc.vector.tensor_copy(mid[64:96, :], rest[64:96, :]))
                v.wait_ge(vec.sem, vec.now)
                vec.done(nc.vector.tensor_tensor(rest[64:96, :], rest[64:96, :], mid[64:96, :], ALU.subtract))
                v.wait_ge(vec.sem, vec.now)
                vec.done(nc.vector.tensor_copy(parts[64:96, at], rest[64:96, :]))
                v.wait_ge(vec.sem, vec.now)
                vec.leave(NB)
            vec.done(nc.vector.memset(a_neg[:, :, N0:N0 + 1], 0.0))
            v.wait_ge(neg_a, 1)
            nc.vector.tensor_scalar(a_neg[:, :, 0:N0], a_neg[:, :, 0:N0], -1.0, None, ALU.mult).then_inc(neg_a, 1)
            one_e = areaB[:, 1024:1536]
            with v.Fori(0, NB) as c:
                vec.enter(c, 10)
                at = bass.ds(c * 512, 512)
                for hf in range(2):
                    v.wait_ge(z_exp, c * 2 + hf + 1)
                    nc.vector.tensor_scalar(delta[:, hf, at], bank[:, 2 + hf, :], b_dt[:, hf:hf + 1], 0.0, ALU.add, ALU.max).then_inc(z_free, 1)
                    vec.done(nc.vector.tensor_scalar(one_e, dx[:, hf, at], 1.0, None, ALU.add))
                    v.wait_ge(z_free, c * 2 + hf + 2 + 1)
                    v.wait_ge(vec.sem, vec.now)
                    vec.done(nc.vector.tensor_tensor(delta[:, hf, at], delta[:, hf, at], y[:, hf, at], ALU.add))
                    vec.done(nc.vector.scalar_tensor_tensor(one_e, one_e, 1.0, dx[:, hf, at], ALU.subtract, ALU.subtract))
                    v.wait_ge(vec.sem, vec.now)
                    vec.done(nc.vector.tensor_tensor(delta[:, hf, at], delta[:, hf, at], one_e, ALU.subtract))
                    v.wait_ge(vec.sem, vec.now)
                    vec.done(nc.vector.tensor_tensor(dx[:, hf, at], delta[:, hf, at], xnT[:, hf, at], ALU.mult))
                vec.leave(NB)

        U0, I0 = 10, NT0 // 10
        assert UN == 8 * I0 and NT0 % 10 == 0

        def fill(i, u, f):
            m = u // 2 + 1
            return i * 2 + m // 2, m % 2, i * 16 + 4 * m + f

        def bc_product(pe, n, bp, count, f):
            pe.wait_ge(bc_ready, count + 1)
            row = n + N0 * (f // 2)
            nc.tensor.matmul(bank[:, f % 2, :], pick[:, bass.ds(row, 1)].to_broadcast([96, P]),
                             parts[:, bp * LB + (f % 2) * 512:bp * LB + (f % 2) * 512 + 512], start=True, stop=True).then_inc(bc_full, 1)

        def bc_copy(act, n, bp, count, f, pair):
            act.wait_ge(bc_full, count + 1)
            if f == 0:
                act.wait_ge(pair_free, pair + 1)
            nc.scalar.activation(bc[:, 2 * bp + f // 2, (f % 2) * 512:(f % 2) * 512 + 512], bank[:, f % 2, :], ACT.Copy).then_inc(bc_ready, 1)

        def decay(act, n, unit, bp, hf):
            act.wait_ge(da_free, unit + 1)
            apart(act)
            view = delta[:, hf, bp * LB:(bp + 1) * LB].rearrange("p (b t) -> p b t", b=2)
            nc.scalar.activation(dA[:, hf, :].rearrange("p (b t) -> p b t", b=2)[:, :, 1:L], view[:, :, 1:L], ACT.Exp,
                                 scale=a_neg[:, hf, bass.ds(n, 1)]).then_inc(da_ready, 1)

        def layer0_tensor(pe):
            pe.wait_ge(s.w_expert, 64)
            for f in range(4):
                bc_product(pe, 0, 0, f, f)
            x_transposes(pe, 0, 0, 0, 1)
            gate_up(pe, 0, 0, 0, wgu0)
            x_transposes(pe, 0, 1, 1, 1)
            with pe.Fori(0, I0) as i:
                for u in range(U0):
                    if u < 8:
                        for f in (2 * (u % 2), 2 * (u % 2) + 1):
                            n, bp, count = fill(i, u, f)
                            bc_product(pe, n, bp, count, f)
                    q = i * U0 + u
                    gate_up(pe, 0, q + 1, (u + 1) % 2, wgu0)
                    product = down(pe, 0, q, u % 2, wd0)
                    x_transposes(pe, 0, q + 2, (u + 2) % 5, i * 2 + (u + 2) // 5 + 1)
                    product()

        def layer0_scalar(act):
            act.wait_ge(y_init, 2)
            act.wait_ge(neg_a, 2)
            for f in range(4):
                bc_copy(act, 0, 0, f, f, 0)
            decay(act, 0, 0, 0, 0)
            xT_copy(act, 0, 0, 0)
            gate_tanh(act, 0, 0, 0)
            xT_copy(act, 0, 1, 1)
            with act.Fori(0, I0) as i:
                for u in range(U0):
                    if u < 8:
                        for f in (2 * (u % 2), 2 * (u % 2) + 1):
                            n, bp, count = fill(i, u, f)
                            bc_copy(act, n, bp, count, f, i * 4 + u // 2 + 1)
                        w = u + 1
                        decay(act, i * 2 + w // 4, i * 8 + w, w // 2 % 2, w % 2)
                    q = i * U0 + u
                    gate_tanh(act, 0, q + 1, (u + 1) % 2)
                    hT_copy(act, 0, q, u % 2)
                    xT_copy(act, 0, q + 2, u % 2)
                    y_copy(act, 0, q, u % 2, u % 5, i * 2 + u // 5 + 1)

        def layer0_vector(v):
            vec.done(nc.vector.memset(dA[:, :, :].rearrange("p r (b t) -> p r b t", b=2)[:, :, :, 0:1], 0.0))
            for hf in range(2):
                nc.vector.tensor_scalar(y[:, hf, :], xnT[:, hf, :], d_par[:, hf:hf + 1], None, ALU.mult).then_inc(y_init, 1)
            v.wait_ge(vec.sem, vec.now)
            v.wait_ge(y_init, 2)
            silu_first(v, 0, 0, 0)
            v.wait_ge(vec.sem, vec.now)
            silu_second(v, 0, 0, 0)
            with v.Fori(0, I0) as i:
                vec.enter(i, 8 * 3 + U0)
                for u in range(U0):
                    q = i * U0 + u
                    nn, bp, hf = u // 4, u // 2 % 2, u % 2
                    if u < 8:
                        v.wait_ge(bc_ready, i * 16 + 4 * (u // 2) + 4 + 2)
                        bx = vec.done(nc.vector.tensor_tensor(h, dx[:, hf, bp * LB:(bp + 1) * LB], bc[:, 2 * bp, :], ALU.mult))
                    silu_first(v, 0, q + 1, (u + 1) % 2)
                    first = vec.now
                    if u < 8:
                        v.wait_ge(da_ready, i * 8 + u + 1)
                        v.wait_ge(vec.sem, bx)
                        nc.vector.tensor_tensor_scan(h, dA[:, hf, :], h, 0.0, ALU.mult, ALU.add).then_inc(da_free, 1)
                    v.wait_ge(vec.sem, first)
                    silu_second(v, 0, q + 1, (u + 1) % 2)
                    if u < 8:
                        v.wait_ge(da_free, i * 8 + u + 1 + 2)
                        hc = vec.done(nc.vector.tensor_tensor(h, h, bc[:, 2 * bp + 1, :], ALU.mult))
                        v.wait_ge(vec.sem, hc)
                        if hf == 1:
                            nc.vector.sem_inc(pair_free, 1)
                        yp = y[:, hf, bp * LB:(bp + 1) * LB]
                        vec.done(nc.vector.tensor_tensor(yp, yp, h, ALU.add))
                        v.wait_ge(vec.sem, vec.now)
                vec.leave(I0)
            nc.vector.sem_inc(s.experts_done, 1)

        def layer0_sync(sp):
            with sp.Fori(0, I0) as i:
                for u in range(U0):
                    y_store(sp, 0, i * U0 + u, u % 5)

        def combine_pool(pool, l, K, n_tiles, rows):
            s = ly[l]
            pool.wait_ge(s.experts_done, 1)
            for slot in range(RING[l]):
                pool.wait_ge(s.stored[slot], 16 * (n_tiles // RING[l] + 1))
            for t in range(TT):
                if t >= 4:
                    pool.wait_ge(s.y_sum, t - 3)
                for k in range(K):
                    nc.gpsimd.indirect_dma_start(rows[:, t % 4, k, :], None, y_d[l],
                                                 bass.IndirectOffsetOnAxis(ap=slot_i[:, t, k:k + 1], axis=0)).then_inc(s.rows[t % 4], 16)

        def combine_vector(v, l, K, rows):
            s = ly[l]
            for t in range(TT):
                v.wait_ge(s.rows[t % 4], 16 * K * (t // 4 + 1))
                for k in range(K):
                    last = nc.vector.scalar_tensor_tensor(x0[:, t, :], rows[:, t % 4, k, :], weight[:, t, k:k + 1], x0[:, t, :],
                                                          ALU.mult, ALU.add)
                    if k < K - 1:
                        vec.done(last)
                        v.wait_ge(vec.sem, vec.now)
                last.then_inc(s.y_sum, 1)

        def scan_out_tensor(pe):
            pe.wait_ge(s.experts_done, 1)
            for t in range(TT):
                if t >= 2:
                    pe.wait_ge(yT_free, t - 1)
                for hf in range(2):
                    last = nc.tensor.transpose(bank[:, t % 2, hf * P:(hf + 1) * P], y[:, hf, t * P:(t + 1) * P], ident[:, :])
                last.then_inc(yT_full, 1)

        def scan_out_vector(v):
            for t in range(TT):
                v.wait_ge(yT_full, t + 1)
                nc.vector.tensor_tensor(x0[:, t, :], bank[:, t % 2, 0:D], x0[:, t, :], ALU.add).then_inc(yT_free, 1)
            v.wait_ge(yT_free, TT)

    HEADS, HD, NS, C1, Q = 64, 8, 128, 768, 64
    DI = HEADS * HD
    NEVER = -1e38
    G1 = DI // P
    HP = HEADS // 2
    CH = L // Q
    PAIRS = CH // 2
    with ExitStack() as c1a, ExitStack() as c1:
        q1 = ly[1]
        areaA1 = sb("areaA1", [P, (KD * 2 * FI + 2 * D) * E], F32, c1a)
        wgu1 = areaA1[:, 0:KD * E * 2 * FI].rearrange("p (k e f) -> p k e f", k=KD, e=E)
        wd1 = areaA1[0:FH, KD * E * 2 * FI:].rearrange("p (h e d) -> p h e d", h=2, e=E)
        xn_tok1 = areaA1[:, 0:TT * D].rearrange("p (t d) -> p t d", t=TT)
        m1 = route_memory(areaA1[:, TT * D:], 1, K1, E)
        F1 = -(-SI1 // P)
        wr1 = sb("wr1", [P, KD, E], F32, c1a)
        sg1 = sb("sg1", [P, KD, F1 * P], F32, c1a)
        su1 = sb("su1", [P, KD, F1 * P], F32, c1a)
        sd1 = sb("sd1", [P, F1, D], F32, c1a)
        shT1 = sb("shT1", [P, F1, 512], F32, c1a)
        th1 = sb("th1", [P, 2, 512], F32, c1a)
        c1a.close()

        w_in = sb("w_in", [P, KD, DI + C1], F32, c1)
        w_dt1 = sb("w_dt1", [P, KD, 2, 3, HP], F32, c1)
        w_out = sb("w_out", [P, G1, D], F32, c1)
        norm_w = sb("norm_w", [P, G1], F32, c1)
        d_head = sb("d_head", [P, G1], F32, c1)
        conv_w = sb("conv_w", [P, C1 // P, 4], F32, c1)
        conv_b = sb("conv_b", [P, C1 // P], F32, c1)
        dt_b = sb("dt_b", [96, 2], F32, c1)
        a1 = sb("a1", [96, 2], F32, c1)
        restart = sb("restart", [96, L], F32, c1)
        sel_c = sb("sel_c", [Q + 6, P], BF16, c1)
        minus_pick = sb("minus_pick", [96, HP, Q], BF16, c1)
        xpad = sb("xpad", [P, 2, 3 + L], F32, c1)
        cv = sb("cv", [P, 2, L], F32, c1)
        tb = sb("tb", [P, 2, L], F32, c1)
        xb2 = sb("xb2", [P, G1 + 1, CH, 2, Q], F32, c1)
        xB = xb2[:, G1, :, :, :]
        xC = sb("xC", [P, L], F32, c1)
        sq = xb2[:, 0:G1, :, :, :].rearrange("p g k r t -> p g (k r t)")[:, :, 0:L]
        gz = sb("gz", [P, G1, L], F32, c1)
        dtT_c = sb("dtT_c", [96, CH, 2, Q], F32, c1)
        e1 = sb("e1", [96, 2, L], F32, c1)
        l1_c = sb("l1_c", [96, CH, 2, Q], F32, c1)
        cT = sb("cT", [96, 2, L], F32, c1)
        rest1 = sb("rest1", [96, 2, L], F32, c1)
        mid1 = sb("mid1", [96, 2, L], BF16, c1)
        cp_c = sb("cp_c", [96, CH, 2, Q], BF16, c1)
        dtT, l1, cp = (v[:, :, :, :].rearrange("p k h t -> p h k t") for v in (dtT_c, l1_c, cp_c))

        def hk(v, hf=None):
            return (v[:, :, :] if hf is None else v[:, hf:hf + 1, :]).rearrange("p h (k t) -> p h k t", t=Q)

        crow = sb("crow", [Q + 6, 2, HP, Q], BF16, c1)
        dw = sb("dw", [P, 2, CH, HP], F32, c1)
        ecn = sb("ecn", [P, PAIRS, HEADS], F32, c1)
        diag = sb("diag", [HP, CH, HEADS], F32, c1)
        dec = sb("dec", [P, CH, HEADS], F32, c1)
        S = sb("S", [P, DI], F32, c1)
        gb = sb("gb", [P, 2, Q + P], F32, c1)
        xq = sb("xq", [P, 2, HP, 2, HD], F32, c1)
        xd = sb("xd", [P, 2, G1, 2, 8, HD], F32, c1)
        ex = sb("ex", [P, 2, 512], F32, c1)
        mm = sb("mm", [P, 4, 512], F32, c1)
        ys = sb("ys", [P, DI], F32, c1)
        y2 = sb("y2", [P, G1, P], F32, c1)
        hg = sb("hg", [P, G1, L], F32, c1)
        rows1 = sb("rows1", [P, 4, K1, D], F32, c1)
        rs = sb("rs", [P, 4, PAIRS], F32, c1)
        cp_d = nc.dram_tensor("cp_d", (NB, 2, 3, HP, L), BF16).ap()

        w_ssd, w_ssd_ready, consts1 = sem("w_ssd"), sem("w_ssd_ready"), sem("consts1")
        dt_z, dt_sum, dt_exp, w_ready, diag_ready, cp_ready, cp_stored = (
            sem(n) for n in ("dt_z", "dt_sum", "dt_exp", "w_ready", "diag_ready", "cp_ready", "cp_stored"))
        conv_sum, conv_tanh, conv_out, gate_th = (sem(n) for n in ("conv_sum", "conv_tanh", "conv_out", "gate_th"))
        xt_full, xt_used, st_full, s_ready, yo_full, m_ready, m_used = (
            sem(n) for n in ("xt_full", "xt_used", "st_full", "s_ready", "yo_full", "m_ready", "m_used"))
        y_tok, hg_ready, sq_ready, ssq_out = (sem(n) for n in ("y_tok", "hg_ready", "sq_ready", "ssq_out"))
        crow_in = [sem(f"crow_in{k}") for k in range(2)]
        ring_full = [sem(f"ring_full{k}") for k in range(2)]
        ring_free = [sem(f"ring_free{k}") for k in range(2)]

        CONV_ORDER = (4, 5, 0, 1, 2, 3)
        PIECES = ([("dt", 0), ("dt", 1)] + [("conv", j) for j in CONV_ORDER] + [("gate", g) for g in range(G1)]
                  + ["dw", "ec", "dec"])
        for step in range(CH + 2):
            if step < CH:
                PIECES.append(("gb", step))
            if step % 2 and step > 1:
                PIECES.append(("yt", (step - 2) // 2))
            if step < CH:
                PIECES += [("seg", step, g) for g in range(G1)]
        PIECES += ["ssq"] + [("out", t) for t in range(PAIRS)]
        NP_ = len(PIECES)
        assert NP_ % 2 == 0
        AT = {name: n for n, name in enumerate(PIECES)}

        def make(pe, b, name):
            k, n = AT[name] % 2, b * (NP_ // 2) + AT[name] // 2
            pe.wait_ge(ring_free[k], n + 1)
            return bank[:, k, :], ring_full[k]

        def take(eng, b, name):
            k, n = AT[name] % 2, b * (NP_ // 2) + AT[name] // 2
            eng.wait_ge(ring_full[k], n + 1)
            return bank[:, k, :], ring_free[k]

        def taken(eng, b, name):
            k, n = AT[name] % 2, b * (NP_ // 2) + AT[name] // 2
            eng.wait_ge(ring_free[k], n + 2)

        def state_of(eng, b, chunk):
            eng.wait_ge(s_ready, b * (CH + 1) + chunk + 1)

        def chunk_past(eng, b, step):
            state_of(eng, b, max(step - 1, 0))

        def experts1_tensor(pe):
            pe.wait_ge(q1.w_expert, 64)
            x_transposes(pe, 1, 0, 0, 1)
            gate_up(pe, 1, 0, 0, wgu1)
            x_transposes(pe, 1, 1, 1, 1)
            with pe.Fori(0, NT1 // 8) as i:
                for u in range(8):
                    q = i * 8 + u
                    gate_up(pe, 1, q + 1, (u + 1) % 2, wgu1)
                    product = down(pe, 1, q, u % 2, wd1)
                    x_transposes(pe, 1, q + 2, (u + 2) % 4, i * 2 + (u + 2) // 4 + 1)
                    product()

        def experts1_scalar(act):
            xT_copy(act, 1, 0, 0)
            gate_tanh(act, 1, 0, 0)
            xT_copy(act, 1, 1, 1)
            with act.Fori(0, NT1 // 8) as i:
                for u in range(8):
                    q = i * 8 + u
                    gate_tanh(act, 1, q + 1, (u + 1) % 2)
                    hT_copy(act, 1, q, u % 2)
                    xT_copy(act, 1, q + 2, u % 2)
                    y_copy(act, 1, q, u % 2, u % 4, i * 2 + u // 4 + 1)

        def experts1_vector(v):
            silu_first(v, 1, 0, 0)
            v.wait_ge(vec.sem, vec.now)
            silu_second(v, 1, 0, 0)
            with v.Fori(0, NT1 // 8) as i:
                vec.enter(i, 8)
                for u in range(8):
                    silu_first(v, 1, i * 8 + u + 1, (u + 1) % 2)
                    v.wait_ge(vec.sem, vec.now)
                    silu_second(v, 1, i * 8 + u + 1, (u + 1) % 2)
                vec.leave(NT1 // 8)
            nc.vector.sem_inc(q1.experts_done, 1)

        def experts1_sync(sp):
            with sp.Fori(0, NT1 // 8) as i:
                for u in range(8):
                    y_store(sp, 1, i * 8 + u, u % 4)

        def experts1_past(eng):
            eng.wait_ge(q1.y_ready, NT1 + 2)

        def scan1_constants(pool):
            experts1_past(pool)
            poo.done(nc.gpsimd.memset(restart[:, :], 1.0))
            poo.done(nc.gpsimd.memset(sel_c[:, :], 0.0))
            poo.done(nc.gpsimd.memset(crow[0:Q, :, :, :], 0.0))
            poo.done(nc.gpsimd.memset(minus_pick[:, :, :], 0.0))
            poo.done(nc.gpsimd.memset(xpad[:, :, 0:3], 0.0))
            poo.done(nc.gpsimd.memset(xq[:, :, :, :, :], 0.0))
            poo.done(nc.gpsimd.memset(xd[:, :, :, :, :, :], 0.0))
            pool.wait_ge(poo.sem, poo.now)
            poo.done(nc.gpsimd.memset(restart[:, :].rearrange("p (k t) -> p k t", t=Q)[:, :, 0:1], 0.0))
            poo.done(nc.gpsimd.affine_select(out=crow[0:Q, :, :, :], in_=crow[0:Q, :, :, :], compare_op=ALU.is_ge, fill=NEVER,
                                             base=0, pattern=[[0, 2 * HP], [1, Q]], channel_multiplier=-1))
            poo.done(nc.gpsimd.affine_select(out=sel_c[:, :], in_=sel_c[:, :], compare_op=ALU.not_equal, fill=1.0,
                                             base=0, pattern=[[0, 2], [-1, Q]], channel_multiplier=1))
            pool.wait_ge(poo.sem, poo.now)
            for part in range(3):
                poo.done(nc.gpsimd.affine_select(out=minus_pick[:, :, :], in_=minus_pick[:, :, :], compare_op=ALU.not_equal,
                                                 fill=-1.0, base=-part * HP, pattern=[[-1, HP], [0, Q]], channel_multiplier=1))
                poo.done(nc.gpsimd.affine_select(out=sel_c[:, :], in_=sel_c[:, :], compare_op=ALU.not_equal, fill=1.0,
                                                 base=-(Q + part), pattern=[[-3, 2], [0, Q]], channel_multiplier=1))
                pool.wait_ge(poo.sem, poo.now)
            pool.sem_inc(consts1, 1)

        W_SSD = 16 * 9

        def scan1_sync(sp):
            experts1_past(sp)
            for to, src in ((w_in[:, :, :], a["w_in1"].rearrange("(k p) n -> p k n", p=P)),
                            (w_dt1[:, :, :, :, :].rearrange("p k h r n -> p k (h r n)"), a["w_dt1"].rearrange("(k p) n -> p k n", p=P)),
                            (w_out[:, :, :], a["w_out1"].rearrange("(g p) d -> p g d", p=P)),
                            (norm_w[:, :], a["norm_w"]), (d_head[:, :], a["d_head"]),
                            (conv_w[:, :, :].rearrange("p j i -> p (j i)"), a["conv_w"]), (conv_b[:, :], a["conv_b"]),
                            (dt_b[:, :], a["dt_b1"]), (a1[:, :], a["a_log1"])):
                sp.dma_start(to, src).then_inc(w_ssd, 16)
            with sp.Fori(0, NB) as b:
                sp.wait_ge(cp_ready, b + 1)
                for hf in range(2):
                    sp.dma_start(cp_d[bass.ds(b, 1), hf, :, :, :].rearrange("a r n (k t) -> (a r n) k t", t=Q), cp_c[:, :, hf, :]).then_inc(cp_stored, 16)
                sp.wait_ge(cp_stored, b * 32 + 32)
                for kk in range(CH):
                    chunk_past(sp, b, kk)
                    sp.dma_start(crow[Q:, kk % 2, :, :], cp_d[bass.ds(b, 1), :, :, :, kk * Q:(kk + 1) * Q].rearrange("a h r n t -> (a h r) n t")
                                 ).then_inc(crow_in[kk % 2], 16)

        def scan1_tensor(pe):
            pe.wait_ge(w_ssd, W_SSD)
            pe.wait_ge(w_ssd_ready, 2)
            pe.wait_ge(consts1, 1)
            with pe.Fori(0, NB) as b:
                def project(name, rows, w):
                    o, full = make(pe, b, name)
                    for k in range(KD):
                        last = nc.tensor.matmul(o[0:rows, :], w(k), xnT[:, k, bass.ds(b * L, L)], start=(k == 0), stop=(k == KD - 1))
                    last.then_inc(full, 1)

                for hf in range(2):
                    project(("dt", hf), 96, lambda k: w_dt1[:, k, hf, :, :].rearrange("p r n -> p (r n)"))
                for j in CONV_ORDER:
                    project(("conv", j), P, lambda k: w_in[:, k, DI + j * P:DI + (j + 1) * P])
                for g in range(G1):
                    project(("gate", g), P, lambda k: w_in[:, k, g * P:(g + 1) * P])
                o, full = make(pe, b, "dw")
                pe.wait_ge(w_ready, b + 1)
                apart(pe)
                for n, src in enumerate((dtT_c, l1_c)):
                    for kk in range(CH):
                        last = nc.tensor.transpose(o[:, (n * CH + kk) * HP:(n * CH + kk + 1) * HP],
                                                   src[0:HP, kk, :, :].rearrange("p h t -> p (h t)"), ident[0:HP, 0:HP])
                last.then_inc(full, 1)
                o, full = make(pe, b, "ec")
                apart(pe)
                for t in range(PAIRS):
                    for hf in range(2):
                        last = nc.tensor.transpose(o[:, (t * 2 + hf) * HP:(t * 2 + hf + 1) * HP],
                                                   e1[0:HP, hf, t * P:(t + 1) * P], ident[0:HP, 0:HP])
                last.then_inc(full, 1)
                o, full = make(pe, b, "dec")
                pe.wait_ge(diag_ready, b * 2 + 2)
                nc.tensor.matmul(o[:, :], ones[0:HP, :], diag[:, :, :].rearrange("p k h -> p (k h)"), start=True, stop=True).then_inc(full, 1)

                pe.wait_ge(conv_out, b * 6 + 6 + 2)
                for step in range(CH + 2):
                    old = step - 1
                    at = slice(step * Q, (step + 1) * Q)
                    if step < CH:
                        o, full = make(pe, b, ("gb", step))
                        Bt, Ct = xB[:, step, :, :].rearrange("p r t -> p (r t)"), xC[:, at]
                        nc.tensor.matmul(o[:, 0:Q], Bt, Ct, start=True, stop=True)
                        nc.tensor.transpose(o[:, Q:Q + P], Bt, ident[:, :]).then_inc(full, 1)
                        for g in range(G1):
                            last = nc.tensor.transpose(bank[:, 5 + step % 2, g * P:(g + 1) * P],
                                                       xb2[:, g, step, :, :].rearrange("p r t -> p (r t)"), ident[:, :])
                        last.then_inc(xt_full, 1)
                    if 0 < step <= CH:
                        taken(pe, b, ("gb", old))
                        pe.wait_ge(xt_used, b * CH + old + 1)
                        nc.tensor.matmul(bank[:, 2, :], gb[:, old % 2, Q:Q + P],
                                         xd[:, old % 2, :, :, :, :].rearrange("p g h j d -> p (g h j d)"), start=True, stop=True).then_inc(st_full, 1)
                    if step % 2 and step > 1:
                        pair = (step - 2) // 2
                        o, full = make(pe, b, ("yt", pair))
                        pe.wait_ge(y_tok, b * PAIRS + pair + 1)
                        for g in range(G1):
                            last = nc.tensor.transpose(o[:, g * P:(g + 1) * P], ys[:, g * P:(g + 1) * P], ident[:, :])
                        last.then_inc(full, 1)
                    for g in range(G1):
                        if step < CH:
                            if g == 0:
                                pe.wait_ge(crow_in[step % 2], b * (8 * CH) + (step // 2 + 1) * 16)
                            o, full = make(pe, b, ("seg", step, g))
                            nc.tensor.matmul(o[:, :], sel_c[:, :], crow[:, step % 2, 8 * g:8 * g + 8, :].rearrange("p j t -> p (j t)"),
                                             start=True, stop=False)
                            nc.tensor.matmul(o[:, :], cp_c[:, step, :, :].rearrange("p h t -> p (h t)"), minus_pick[:, 8 * g:8 * g + 8, :].rearrange("p j t -> p (j t)"),
                                             start=False, stop=True).then_inc(full, 1)
                        if 0 < step <= CH:
                            pe.wait_ge(m_ready, b * (CH * G1) + old * G1 + g + 1 + 2)
                            r = (old % 2) * Q
                            for j in range(8):
                                to = bank[r:r + Q, 4, g * P:(g + 1) * P].rearrange("p (h j d) -> p h j d", h=2, j=8)[:, :, j, :]
                                last = nc.tensor.matmul(to, mm[:, g, j * Q:(j + 1) * Q], xq[:, old % 2, 8 * g + j, :, :].rearrange("p h d -> p (h d)"),
                                                        start=True, stop=True)
                            last.then_inc(m_used, 1)
                    if step < CH:
                        state_of(pe, b, step)
                        r = (step % 2) * Q
                        nc.tensor.matmul(bank[r:r + Q, 3 + 4 * (step // 2 % 2), :], Ct, S[:, :], start=True, stop=True).then_inc(yo_full, 1)
                o, full = make(pe, b, "ssq")
                pe.wait_ge(sq_ready, b + 1)
                for t in range(PAIRS):
                    for g in range(G1):
                        last = nc.tensor.matmul(o[:, 2 * t:2 * t + 2], sq[:, g, t * P:(t + 1) * P], ones[:, 0:2], start=(g == 0), stop=(g == G1 - 1))
                last.then_inc(full, 1)
                for t in range(PAIRS):
                    o, full = make(pe, b, ("out", t))
                    for g in range(G1):
                        last = nc.tensor.matmul(o[:, 0:D], hg[:, g, t * P:(t + 1) * P], w_out[:, g, :], start=(g == 0), stop=(g == G1 - 1))
                    last.then_inc(full, 1)

        def scan1_scalar(act):
            act.wait_ge(w_ssd, W_SSD)
            nc.scalar.activation(a1[:, :], a1[:, :], ACT.Exp).then_inc(w_ssd_ready, 1)
            act.wait_ge(w_ssd_ready, 2)
            act.wait_ge(consts1, 1)
            with act.Fori(0, NB) as b:
                sca.enter(b, 3)
                for hf in range(2):
                    o, free = take(act, b, ("dt", hf))
                    nc.scalar.activation(dtT[:, hf, :, :], o[0:96, :].rearrange("p (k t) -> p k t", t=Q), ACT.Identity, bias=dt_b[:, hf:hf + 1]).then_inc(free, 1)
                for hf in range(2):
                    taken(act, b, ("dt", hf))
                sca.done(nc.scalar.activation(l1_c[:, :, :, :], dtT_c[:, :, :, :], ACT.Abs))
                act.wait_ge(sca.sem, sca.now)
                sca.done(nc.scalar.activation(hk(e1), l1, ACT.Exp, scale=-1.0))
                act.wait_ge(sca.sem, sca.now)
                nc.scalar.activation(l1, hk(e1), ACT.Ln, bias=1.0).then_inc(dt_z, 1)

                def tanh_of(n):
                    act.wait_ge(conv_sum, b * 6 + n + 1)
                    nc.scalar.activation(tb[:, n % 2, :], cv[:, n % 2, :], ACT.Tanh).then_inc(conv_tanh, 1)

                for n, j in enumerate(CONV_ORDER):
                    o, free = take(act, b, ("conv", j))
                    act.wait_ge(conv_out, b * 6 + n + 1)
                    nc.scalar.activation(xpad[:, n % 2, 3:], o, ACT.Copy)
                    nc.scalar.activation(cv[:, n % 2, :], o, ACT.Identity, scale=conv_w[:, j, 3:4],
                                         bias=conv_b[:, j:j + 1]).then_inc(free, 1)
                    if n:
                        tanh_of(n - 1)
                tanh_of(5)
                for g in range(G1):
                    o, free = take(act, b, ("gate", g))
                    if g < 2:
                        act.wait_ge(conv_out, b * 6 + 5 + g + 2)
                    else:
                        taken(act, b, ("gate", g - 2))
                    nc.scalar.activation(tb[:, g % 2, :], o, ACT.Tanh, scale=0.5).then_inc(gate_th, 1)
                act.wait_ge(dt_sum, b + 1)
                nc.scalar.activation(e1[:, :, :], cT[:, :, :], ACT.Exp).then_inc(dt_exp, 1)
                nc.scalar.activation(l1_c[:, :, :, :], l1_c[:, :, :, :], ACT.Exp).then_inc(dt_exp, 1)
                act.wait_ge(hg_ready, b * PAIRS + 1)
                o, free = take(act, b, "dw")
                nc.scalar.activation(dw[:, :, :, :].rearrange("p n k h -> p (n k h)"), o, ACT.Copy).then_inc(free, 1)
                o, free = take(act, b, "ec")
                for hf in range(2):
                    last = None
                    for t in range(PAIRS):
                        src = o[:, (t * 2 + hf) * HP:(t * 2 + hf + 1) * HP].rearrange("p (g j) -> p g j", g=G1)
                        last = nc.scalar.activation(ecn[:, t, :].rearrange("p (g h j) -> p g h j", g=G1, h=2)[:, :, hf, :], src, ACT.Copy)
                last.then_inc(free, 1)
                o, free = take(act, b, "dec")
                nc.scalar.activation(dec[:, :, :].rearrange("p k h -> p (k h)"), o, ACT.Copy).then_inc(free, 1)
                for step in range(CH):
                    o, free = take(act, b, ("gb", step))
                    chunk_past(act, b, step)
                    nc.scalar.activation(gb[:, step % 2, :], o[:, 0:Q + P], ACT.Copy).then_inc(free, 1)
                    for g in range(G1):
                        o, free = take(act, b, ("seg", step, g))
                        act.wait_ge(m_ready, b * (CH * G1) + step * G1 + g + 1)
                        nc.scalar.activation(ex[:, g % 2, :], o, ACT.Exp).then_inc(free, 1)
                act.wait_ge(hg_ready, b * PAIRS + PAIRS + 1)
                nc.scalar.activation(sq, hg[:, :, :], ACT.Square).then_inc(sq_ready, 1)
                taken(act, b, "ssq")
                sca.done(nc.scalar.activation(rs[:, 1, :], rs[:, 0, :], ACT.Ln))
                act.wait_ge(sca.sem, sca.now)
                nc.scalar.activation(rs[:, 2, :], rs[:, 1, :], ACT.Exp, scale=-0.5).then_inc(ssq_out, 1)
                sca.leave(NB)

        def scan1_vector(v):
            v.wait_ge(w_ssd, W_SSD)
            v.wait_ge(w_ssd_ready, 1)
            vec.done(nc.vector.tensor_scalar(conv_w[:, :, :], conv_w[:, :, :], 0.5, None, ALU.mult))
            vec.done(nc.vector.tensor_scalar(conv_b[:, :], conv_b[:, :], 0.5, None, ALU.mult))
            vec.done(nc.vector.tensor_scalar(a1[:, :], a1[:, :], -1.0, None, ALU.mult))
            for g in range(G1):
                vec.done(nc.vector.tensor_scalar(w_out[:, g, :], w_out[:, g, :], norm_w[:, g:g + 1], None, ALU.mult))
            v.wait_ge(vec.sem, vec.now)
            v.sem_inc(w_ssd_ready, 1)
            v.wait_ge(consts1, 1)
            with v.Fori(0, NB) as b:
                vec.enter(b, 41)

                def step_done(ins):
                    vec.done(ins)
                    v.wait_ge(vec.sem, vec.now)

                v.wait_ge(dt_z, b + 1)
                vec.done(nc.vector.scalar_tensor_tensor(dtT_c[:, :, :, :], dtT_c[:, :, :, :], 0.0, l1_c[:, :, :, :], ALU.max, ALU.add))
                step_done(nc.vector.tensor_scalar(rest1[:, :, :], e1[:, :, :], 1.0, None, ALU.add))
                step_done(nc.vector.scalar_tensor_tensor(rest1[:, :, :], rest1[:, :, :], 1.0, e1[:, :, :], ALU.subtract, ALU.subtract))
                step_done(nc.vector.tensor_tensor(dtT, dtT, hk(rest1), ALU.subtract))
                for hf in range(2):
                    vec.done(nc.vector.tensor_scalar(hk(rest1, hf), dtT[:, hf:hf + 1, :, :], a1[:, hf:hf + 1], None, ALU.mult))
                v.wait_ge(vec.sem, vec.now)
                for hf in range(2):
                    vec.done(nc.vector.tensor_tensor_scan(cT[:, hf, :], restart[:, :], rest1[:, hf, :], 0.0, ALU.mult, ALU.add))
                v.wait_ge(vec.sem, vec.now)
                for hf in range(2):
                    by_chunk = cT[:, hf, :].rearrange("p (k t) -> p k t", t=Q)
                    last = nc.vector.tensor_tensor(l1[:, hf, :, :],
                                                   by_chunk[:, :, Q - 1:Q].to_broadcast([96, CH, Q]), by_chunk, ALU.subtract)
                last.then_inc(dt_sum, 1)
                step_done(nc.vector.tensor_copy(cp, hk(cT)))
                step_done(nc.vector.tensor_tensor(hk(rest1), hk(cT), cp, ALU.subtract))
                vec.done(nc.vector.tensor_copy(cp[32:64], hk(rest1)[32:64]))
                step_done(nc.vector.tensor_copy(mid1[64:96, :, :], rest1[64:96, :, :]))
                step_done(nc.vector.tensor_tensor(rest1[64:96, :, :], rest1[64:96, :, :], mid1[64:96, :, :], ALU.subtract))
                nc.vector.tensor_copy(cp[64:96], hk(rest1)[64:96]).then_inc(cp_ready, 1)

                def silu_of(n, j):
                    v.wait_ge(conv_tanh, b * 6 + n + 1)
                    if j == 5:
                        places = [xC[:, :].rearrange("p (k t) -> p k t", t=Q)]
                    else:
                        places = [xb2[:, j, :, r, :] for r in range(2)]
                    for to in places:
                        last = nc.vector.scalar_tensor_tensor(to, hk(tb, n % 2)[:, 0], 1.0, hk(cv, n % 2)[:, 0], ALU.add, ALU.mult)
                    last.then_inc(conv_out, 1)

                for n, j in enumerate(CONV_ORDER):
                    taken(v, b, ("conv", j))
                    for i in range(3):
                        last = nc.vector.scalar_tensor_tensor(cv[:, n % 2, :], xpad[:, n % 2, i:i + L], conv_w[:, j, i:i + 1],
                                                              cv[:, n % 2, :], ALU.mult, ALU.add)
                        if i < 2:
                            step_done(last)
                    last.then_inc(conv_sum, 1)
                    if n:
                        silu_of(n - 1, CONV_ORDER[n - 1])
                silu_of(5, CONV_ORDER[5])
                for g in range(G1):
                    o, free = take(v, b, ("gate", g))
                    v.wait_ge(gate_th, b * G1 + g + 1)
                    nc.vector.scalar_tensor_tensor(gz[:, g, :], tb[:, g % 2, :], 1.0, o, ALU.add, ALU.mult).then_inc(free, 1)
                v.wait_ge(dt_exp, b * 2 + 2)
                nc.vector.tensor_tensor(l1_c[0:HP], l1_c[0:HP], dtT_c[0:HP], ALU.mult).then_inc(w_ready, 1)
                for hf in range(2):
                    ends = e1[0:HP, hf, :].rearrange("p (k t) -> p k t", t=Q)[:, :, Q - 1:Q]
                    to = diag[:, :, :].rearrange("p k (g h j) -> p k g h j", g=G1, h=2)[:, :, :, hf, :]
                    for g in range(G1):
                        last = nc.vector.tensor_tensor(to[:, :, g, :], ends.to_broadcast([HP, CH, 8]),
                                                       ident[0:HP, None, 8 * g:8 * g + 8].to_broadcast([HP, CH, 8]), ALU.mult)
                    last.then_inc(diag_ready, 1)
                nc.vector.memset(S[:, :], 0.0).then_inc(s_ready, 1)
                for name in ("dw", "ec", "dec"):
                    taken(v, b, name)
                for step in range(CH + 2):
                    old = step - 1
                    if step < CH:
                        v.wait_ge(xt_full, b * CH + step + 1)
                        for n in range(2):
                            for hf in range(2):
                                r = slice(hf * Q, (hf + 1) * Q)
                                x_half = bank[r, 5 + step % 2, :].rearrange("p (g h j d) -> p g h j d", g=G1, h=2, j=8)[:, :, hf, :, :]
                                to = (xq[r, step % 2, :, hf, :].rearrange("p (g j) d -> p g j d", g=G1), xd[r, step % 2, :, hf, :, :])[n]
                                last = nc.vector.tensor_tensor(to, x_half,
                                                               dw[r, n, step, :].rearrange("p (g j) -> p g j", g=G1).unsqueeze(3)
                                                               .to_broadcast([Q, G1, 8, HD]), ALU.mult)
                        last.then_inc(xt_used, 1)
                    if 0 < step <= CH:
                        v.wait_ge(yo_full, b * CH + old + 1)
                        s3 = S[:, :].rearrange("p (h d) -> p h d", d=HD)
                        if old:
                            state_of(v, b, old)
                        step_done(nc.vector.tensor_tensor(s3, s3, dec[:, old, :].unsqueeze(2).to_broadcast([P, HEADS, HD]), ALU.mult))
                        v.wait_ge(st_full, b * CH + old + 1)
                        nc.vector.tensor_tensor(S[:, :], S[:, :], bank[:, 2, :], ALU.add).then_inc(s_ready, 1)
                    if step % 2 and step > 1:
                        t = (step - 2) // 2
                        o, free = take(v, b, ("yt", t))
                        at = slice(t * P, (t + 1) * P)
                        for g in range(G1):
                            last = nc.vector.scalar_tensor_tensor(y2[:, g, :].rearrange("p (k t) -> p k t", t=Q), xb2[:, g, 2 * t:2 * t + 2, 0, :],
                                                                  d_head[:, g:g + 1], o[:, g * P:(g + 1) * P].rearrange("p (k t) -> p k t", t=Q),
                                                                  ALU.mult, ALU.add)
                        last.then_inc(free, 1)
                        taken(v, b, ("yt", t))
                        nc.vector.scalar_tensor_tensor(hg[:, :, at], y2[:, :, :], 0.5, gz[:, :, at], ALU.mult, ALU.mult).then_inc(hg_ready, 1)
                    if step < CH:
                        taken(v, b, ("gb", step))
                        for g in range(G1):
                            taken(v, b, ("seg", step, g))
                            v.wait_ge(m_used, b * (CH * G1) + step * G1 + g + 1)
                            nc.vector.tensor_tensor(mm[:, g, :].rearrange("p (j t) -> p j t", t=Q), ex[:, g % 2, :].rearrange("p (j t) -> p j t", t=Q),
                                                    gb[:, step % 2, 0:Q].unsqueeze(1).to_broadcast([P, 8, Q]), ALU.mult).then_inc(m_ready, 1)
                    if step % 2 == 0 and step > 0:
                        t = old // 2
                        v.wait_ge(m_used, b * (CH * G1) + step * G1 + 4)
                        step_done(nc.vector.tensor_tensor(ys[:, :].rearrange("p (h d) -> p h d", d=HD),
                                                          bank[:, 3 + 4 * (t % 2), :].rearrange("p (h d) -> p h d", d=HD),
                                                          ecn[:, t, :].unsqueeze(2).to_broadcast([P, HEADS, HD]), ALU.mult))
                        nc.vector.tensor_tensor(ys[:, :], ys[:, :], bank[:, 4, :], ALU.add).then_inc(y_tok, 1)
                o, free = take(v, b, "ssq")
                nc.vector.tensor_scalar(rs[:, 0, :], o[:, 0:2 * PAIRS:2], 1.0 / DI, EPS, ALU.mult, ALU.add).then_inc(free, 1)
                v.wait_ge(ssq_out, b + 1)
                r0 = rs[:, 2, :]
                step_done(nc.vector.tensor_tensor(rs[:, 3, :], r0, r0, ALU.mult))
                step_done(nc.vector.tensor_tensor(rs[:, 3, :], rs[:, 3, :], rs[:, 0, :], ALU.mult))
                step_done(nc.vector.tensor_scalar(rs[:, 3, :], rs[:, 3, :], -0.5, 1.5, ALU.mult, ALU.add))
                step_done(nc.vector.tensor_tensor(rs[:, 2, :], r0, rs[:, 3, :], ALU.mult))
                for t in range(PAIRS):
                    o, free = take(v, b, ("out", t))
                    xt = x0[:, bass.ds(b * PAIRS + t, 1), :].rearrange("p a d -> p (a d)")
                    nc.vector.scalar_tensor_tensor(xt, o[:, 0:D], rs[:, 2, t:t + 1], xt, ALU.mult, ALU.add).then_inc(free, 1)
                vec.leave(NB)
            for t in range(2):
                v.wait_ge(ring_free[t], NB * (NP_ // 2) + 1)


        def constants(pool):
            def credit(semaphore, n):
                pool.sem_inc(semaphore, n)

            for q in ly:
                credit(q.sh_free, 2)
                credit(q.sh_pfree, 4)
                credit(q.y_ready, 2)
                for slot in q.stored:
                    credit(slot, 16)
            for semaphore, n in ((row_free, 1), (rank_ready, 1), (z_free, 2), (da_free, 2), (bc_ready, 2), (pair_free, 2)):
                credit(semaphore, n)
            for semaphore, n in ((ring_free[0], 1), (ring_free[1], 1), (conv_out, 2), (m_ready, 2), (m_used, 4), (hg_ready, 1)):
                credit(semaphore, n)
            poo.done(nc.gpsimd.memset(ident[:, :], 0.0))
            poo.done(nc.gpsimd.memset(ones[:, :], 1.0))
            poo.done(nc.gpsimd.memset(not_first[:, :, :], 1.0))
            poo.done(nc.gpsimd.memset(pick[:, :], 0.0))
            pool.wait_ge(poo.sem, poo.now)
            poo.done(nc.gpsimd.affine_select(out=ident[:, :], in_=ident[:, :], compare_op=ALU.not_equal, fill=1.0,
                                             base=0, pattern=[[-1, P]], channel_multiplier=1))
            poo.done(nc.gpsimd.affine_select(out=before[:, :], in_=ones[:, :], compare_op=ALU.is_gt, fill=0.0,
                                             base=0, pattern=[[1, P]], channel_multiplier=-1))
            poo.done(nc.gpsimd.memset(not_first[:, :, 0:1], 0.0))
            for part in range(3):
                poo.done(nc.gpsimd.affine_select(out=pick[:, 0:2 * N0], in_=pick[:, 0:2 * N0], compare_op=ALU.not_equal, fill=1.0,
                                                 base=-part * 2 * N0, pattern=[[-1, 2 * N0]], channel_multiplier=1))
                pool.wait_ge(poo.sem, poo.now)
            poo.done(nc.gpsimd.iota(iota[:, :], [[1, P]], base=0, channel_multiplier=0, allow_small_or_imprecise_dtypes=True))
            poo.done(nc.gpsimd.iota(iota128[:, :], [[P, E]], base=0, channel_multiplier=0, allow_small_or_imprecise_dtypes=True))
            poo.done(nc.gpsimd.iota(token_id[:, :], [[P, TT]], base=0, channel_multiplier=1, allow_small_or_imprecise_dtypes=True))
            pool.wait_ge(poo.sem, poo.now)
            pool.sem_inc(consts_ready, 1)

        def load_experts(dma, l, wgu, wd):
            for k in range(KD):
                dma.dma_start(wgu[:, k, :, :], a[f"gu{l}"][:, k * P:(k + 1) * P, :].rearrange("e p f -> p e f")).then_inc(ly[l].w_expert, 16)
            for h in range(2):
                dma.dma_start(wd[:, h, :, :], a[f"down{l}"][:, h * FH:(h + 1) * FH, :].rearrange("e f d -> f e d")).then_inc(ly[l].w_expert, 16)

        def load0_sync(sp):
            sp.dma_start(x0[:, :, :], a["x"].rearrange("(t p) d -> p t d", p=P)).then_inc(x_loaded, 16)
            wx = a["w_xproj"].rearrange("(k p) e -> p k e", p=P)
            for r in range(3):
                sp.dma_start(wbc[:, :, r, :], wx[:, :, R0:]).then_inc(w_scan, 16)
            sp.dma_start(wdr[:, :, :], wx[:, :, 0:R0]).then_inc(w_scan, 16)
            sp.dma_start(wdt[:, :], a["w_dt"]).then_inc(w_scan, 16)
            sp.dma_start(b_dt[:, :], a["b_dt"]).then_inc(w_scan, 16)
            sp.dma_start(a_neg[:, :, 0:N0], a["a_log0"].rearrange("(h p) n -> p h n", p=P)).then_inc(w_scan, 16)
            sp.dma_start(d_par[:, :], a["d_par"]).then_inc(s.w_router, 16)
            sp.dma_start(wr0[:, :, :], a["gate0"].rearrange("(k p) e -> p k e", p=P)).then_inc(s.w_router, 16)
            layernorm_sync(sp, 0, xn_tok)
            sp.wait_ge(s.mask_ready, 1)
            sp.dma_start(sg0[:, :, 0:SI0], a["sgate0"].rearrange("(k p) f -> p k f", p=P)).then_inc(s.w_shared, 16)
            sp.dma_start(su0[:, :, 0:SI0], a["sup0"].rearrange("(k p) f -> p k f", p=P)).then_inc(s.w_shared, 16)
            full = SI0 // P
            sp.dma_start(sd0[:, 0:full, :], a["sdown0"][0:full * P, :].rearrange("(f p) d -> p f d", p=P)).then_inc(s.w_shared, 16)
            sp.dma_start(sd0[0:SI0 - full * P, full, :], a["sdown0"][full * P:, :]).then_inc(s.w_shared, 16)
            sp.wait_ge(s.indices, 1)
            sp.wait_ge(s.xn_stored, 16)
            sp.wait_ge(s.score2_in, 1)
            load_experts(sp, 0, wgu0, wd0)

        def pads0_vector(v):
            vec.done(nc.vector.memset(sg0[:, :, SI0:], 0.0))
            vec.done(nc.vector.memset(su0[:, :, SI0:], 0.0))
            rest = SI0 % P
            last = nc.vector.memset(sd0[rest:P, F0 - 1, :], 0.0)
            last.then_inc(s.pads, 1)

        def load1_pool(pool):
            pool.wait_ge(q1.xn_rows, 1)
            pool.dma_start(wr1[:, :, :], a["gate1"].rearrange("(k p) e -> p k e", p=P)).then_inc(q1.w_router, 16)
            pool.dma_start(sg1[:, :, 0:SI1], a["sgate1"].rearrange("(k p) f -> p k f", p=P)).then_inc(q1.w_shared, 16)
            pool.dma_start(su1[:, :, 0:SI1], a["sup1"].rearrange("(k p) f -> p k f", p=P)).then_inc(q1.w_shared, 16)
            full = SI1 // P
            pool.dma_start(sd1[:, 0:full, :], a["sdown1"][0:full * P, :].rearrange("(f p) d -> p f d", p=P)).then_inc(q1.w_shared, 16)
            pool.dma_start(sd1[0:SI1 - full * P, full, :], a["sdown1"][full * P:, :]).then_inc(q1.w_shared, 16)
            pool.wait_ge(q1.indices, 1)
            pool.wait_ge(q1.xn_stored, 16)
            load_experts(pool, 1, wgu1, wd1)

        def pads1_vector(v):
            vec.done(nc.vector.memset(sg1[:, :, SI1:], 0.0))
            vec.done(nc.vector.memset(su1[:, :, SI1:], 0.0))
            rest = SI1 % P
            nc.vector.memset(sd1[rest:P, F1 - 1, :], 0.0).then_inc(q1.pads, 1)

        block = ctx.enter_context(nc.Block())

        @block.sync
        def _(sp):
            load0_sync(sp)
            layer0_sync(sp)
            layernorm_sync(sp, 1, xn_tok1)
            experts1_sync(sp)
            scan1_sync(sp)
            sp.wait_ge(q1.y_sum, TT)
            sp.dma_start(out.rearrange("(t p) d -> p t d", p=P), x0[:, :, :]).then_inc(out_stored, 16)
            sp.wait_ge(out_stored, 16)

        @block.gpsimd
        def _(pool):
            constants(pool)
            expert_gather(pool, 0, NT0)
            combine_pool(pool, 0, K0, NT0, rows)
            load1_pool(pool)
            expert_gather(pool, 1, NT1)
            scan1_constants(pool)
            combine_pool(pool, 1, K1, NT1, rows1)

        @block.scalar
        def _(act):
            layernorm_scalar(act, 0)
            scan_rows_scalar(act)
            route_scalar(act, 0, m0)
            act.wait_ge(s.logits, 2)
            nc.scalar.activation(sgate[:, :], m0["logits"][:, :, E], ACT.Exp, scale=-1.0).then_inc(s.score2_in, 1)
            shared_scalar(act, 0, F0, th0)
            layer0_scalar(act)
            layernorm_scalar(act, 1)
            route_scalar(act, 1, m1)
            shared_scalar(act, 1, F1, th1)
            experts1_scalar(act)
            scan1_scalar(act)

        @block.tensor
        def _(pe):
            layernorm_tensor(pe, 0, xn_tok)
            scan_rows_tensor(pe)
            route_tensor(pe, 0, K0, wr0, E + 1, m0)
            shared_tensor(pe, 0, F0, sg0, su0, sd0, shT0)
            layer0_tensor(pe)
            scan_out_tensor(pe)
            layernorm_tensor(pe, 1, xn_tok1)
            route_tensor(pe, 1, K1, wr1, E, m1)
            shared_tensor(pe, 1, F1, sg1, su1, sd1, shT1)
            experts1_tensor(pe)
            scan1_tensor(pe)

        @block.vector
        def _(v):
            v.wait_ge(x_loaded, 16)
            layernorm_vector(v, 0, xn_tok)
            scan_rows_vector(v)
            route_vector(v, 0, K0, E + 1, m0)
            pads0_vector(v)
            v.wait_ge(s.score2_in, 1)
            vec.done(nc.vector.tensor_scalar(sgate[:, :], sgate[:, :], 1.0, None, ALU.add))
            v.wait_ge(vec.sem, vec.now)
            vec.done(nc.vector.reciprocal(sgate[:, :], sgate[:, :]))
            v.wait_ge(vec.sem, vec.now)
            shared_vector(v, 0, F0, th0, shT0, sgate)
            layer0_vector(v)
            scan_out_vector(v)
            combine_vector(v, 0, K0, rows)
            v.wait_ge(s.y_sum, TT)
            layernorm_vector(v, 1, xn_tok1)
            route_vector(v, 1, K1, E, m1)
            pads1_vector(v)
            shared_vector(v, 1, F1, th1, shT1, None)
            experts1_vector(v)
            scan1_vector(v)
            combine_vector(v, 1, K1, rows1)


def kernel(**inputs):
    import concourse.bacc as bacc
    from concourse.bass_utils import run_bass_kernel_spmd

    def last_first(a):
        return np.ascontiguousarray(np.swapaxes(a, -1, -2))

    def columns(a):
        return np.ascontiguousarray(a.reshape(-1, P).T)

    g = {k: np.asarray(v) for k, v in inputs.items()}
    proj = g["L1_attn_in_proj_w"]
    DI, HEADS = 512, 64

    def by_half(v):
        v = v.reshape(4, 2, 8, *v.shape[1:])
        return np.swapaxes(v, 0, 1).reshape(2, 32, *v.shape[3:])

    sgu = g["L0_ffn_shared_gate_up"]
    arrays = dict(
        x=np.ascontiguousarray(g["L0_attn_x"].reshape(T, D)),
        w_xproj=last_first(g["L0_attn_W_xproj"]), w_dt=last_first(g["L0_attn_W_dt"]), b_dt=columns(g["L0_attn_b_dt"]),
        a_log0=g["L0_attn_A_log"], d_par=columns(g["L0_attn_D_param"]),
        gate0=last_first(np.concatenate([g["L0_ffn_gate_w"], g["L0_ffn_shared_gate_vec"]])),
        gu0=last_first(g["L0_ffn_expert_gate_up"]), down0=last_first(g["L0_ffn_expert_down"]),
        sgate0=last_first(sgu[:SI0]), sup0=last_first(sgu[SI0:]), sdown0=last_first(g["L0_ffn_shared_down"]),
        gate1=last_first(g["L1_ffn_gate_w"]),
        gu1=last_first(np.concatenate([g["L1_ffn_w1"], g["L1_ffn_w3"]], axis=1)), down1=last_first(g["L1_ffn_w2"]),
        sgate1=last_first(g["L1_ffn_sw1"]), sup1=last_first(g["L1_ffn_sw3"]), sdown1=last_first(g["L1_ffn_sw2"]),
        w_in1=last_first(proj[:-HEADS]),
        w_dt1=last_first(np.repeat(by_half(proj[-HEADS:])[:, None], 3, axis=1).reshape(6 * 32, D)),
        w_out1=last_first(g["L1_attn_out_proj_w"]), norm_w=columns(g["L1_attn_norm_w"]),
        d_head=columns(np.repeat(g["L1_attn_D"], DI // HEADS)),
        conv_w=np.ascontiguousarray(g["L1_attn_conv_w"].reshape(6, P, 4).transpose(1, 0, 2).reshape(P, 24)),
        conv_b=columns(g["L1_attn_conv_b"]),
        dt_b1=np.ascontiguousarray(np.tile(by_half(g["L1_attn_dt_bias"]).T, (3, 1))),
        a_log1=np.ascontiguousarray(np.tile(by_half(g["L1_attn_A_log"]).T, (3, 1))),
    )
    nc = bacc.Bacc("TRN2", target_bir_lowering=False, num_devices=1)
    aps = {n: nc.dram_tensor(f"in_{n}", v.shape, mybir.dt.from_np(v.dtype), kind="ExternalInput").ap() for n, v in arrays.items()}
    out = nc.dram_tensor("out", (T, D), F32, kind="ExternalOutput").ap()
    build(nc, aps, out)
    r = run_bass_kernel_spmd(nc, [{f"in_{n}": v for n, v in arrays.items()}], core_ids=[0])
    return r.results[0]["out"].reshape(NB, L, D)
```
